# Optimizing a Trainium2 kernel written in Bass

```python
import numpy as np
import jax
import jax.numpy as jnp

def _softmax(x, axis=-1):
    return jax.nn.softmax(x, axis=axis)

def _gelu(x):
    return jax.nn.gelu(x, approximate=True)

def _silu(x):
    return jax.nn.silu(x)

def _sigmoid(x):
    return jax.nn.sigmoid(x)

def _layernorm(x, axis=-1, eps=1e-05):
    m = jnp.mean(x, axis=axis, keepdims=True)
    v = jnp.var(x, axis=axis, keepdims=True)
    return (x - m) / jnp.sqrt(v + eps)

def _scatter_add(tgt, idx, src, axis=0):
    return tgt.at[idx].add(src)

def _segment_sum(src, seg, n):
    return jax.ops.segment_sum(src, seg, n)
kernel_name = 'mk_audio_tower_d1_tok_audfeat512_r4_60b278'

def setup_inputs(seed: int=0):
    np.random.seed(seed)
    _w = jnp.asarray

    def _rec_inputs():
        import jax
        import jax.numpy as jnp
        _rk = jax.random.key(seed)
        x = -0.000292821 + 1.00034 * jax.random.normal(jax.random.fold_in(_rk, 1), (64, 750, 2), jnp.float32)
        return x
    x = _rec_inputs()

    def _L0_tok_setup():
        import jax, jax.numpy as jnp
        import numpy as np
        PATCH_LENGTH = 128
        PATCH_STRIDE = 64
        MODEL_DIM = 128
        LN_EPS = 0.001
        key = jax.random.key(seed)
        k1, k2 = jax.random.split(key)
        B, T, C = (64, 8192, 2)
        x = jax.random.normal(k1, (B, T, C), dtype=jnp.float32)
        in_dim = PATCH_LENGTH * C
        W = jax.random.normal(k2, (in_dim, MODEL_DIM), dtype=jnp.float32) / np.sqrt(in_dim)
        b = jnp.zeros((MODEL_DIM,), dtype=jnp.float32)
        gamma = jnp.ones((MODEL_DIM,), dtype=jnp.float32)
        beta = jnp.zeros((MODEL_DIM,), dtype=jnp.float32)
        return {'x': x, 'W': W, 'b': b, 'gamma': gamma, 'beta': beta}
    _L0_tok_all = _L0_tok_setup()
    _L0_tok_in = {k: v for k, v in _L0_tok_all.items() if k in ('W', 'b', 'gamma', 'beta')}
    del _L0_tok_all

    def _L0_attn_setup():
        import jax, jax.numpy as jnp
        import numpy as np
        DIM = 128
        B, T = (32, 512)

        def _lstm(x, W_ih, W_hh, b_ih, b_hh):
            Bb, Tt, D = x.shape
            xg = jnp.einsum('btd,gd->btg', x, W_ih) + b_ih + b_hh
            xg = jnp.swapaxes(xg, 0, 1)

            def step(carry, xt):
                h, c = carry
                gates = xt + h @ W_hh.T
                i, f, g, o = jnp.split(gates, 4, axis=-1)
                i = jax.nn.sigmoid(i)
                f = jax.nn.sigmoid(f)
                g = jnp.tanh(g)
                o = jax.nn.sigmoid(o)
                c = f * c + i * g
                h = o * jnp.tanh(c)
                return ((h, c), h)
            h0 = jnp.zeros((Bb, D), dtype=x.dtype)
            (_, _), hs = jax.lax.scan(step, (h0, h0), xg)
            return jnp.swapaxes(hs, 0, 1)
        key = jax.random.key(seed)
        k_x, k_wih, k_whh, k_bih, k_bhh = jax.random.split(key, 5)
        s = 1.0 / np.sqrt(DIM)
        return {'x': jax.random.normal(k_x, (B, T, DIM), dtype=jnp.float32), 'W_ih': jax.random.uniform(k_wih, (4 * DIM, DIM), minval=-s, maxval=s, dtype=jnp.float32), 'W_hh': jax.random.uniform(k_whh, (4 * DIM, DIM), minval=-s, maxval=s, dtype=jnp.float32), 'b_ih': jax.random.uniform(k_bih, (4 * DIM,), minval=-s, maxval=s, dtype=jnp.float32), 'b_hh': jax.random.uniform(k_bhh, (4 * DIM,), minval=-s, maxval=s, dtype=jnp.float32)}
    _L0_attn_all = _L0_attn_setup()
    _L0_attn_in = {k: v for k, v in _L0_attn_all.items() if k in ('W_ih', 'W_hh', 'b_ih', 'b_hh')}
    del _L0_attn_all

    def _L0_ffn_setup():
        import jax, jax.numpy as jnp
        import numpy as np
        E = 8
        TOP_K = 2
        D = 128
        H = 256
        B, S = (16, 1024)
        key = jax.random.key(seed)
        ks = jax.random.split(key, 10)
        sd = lambda fan_in: 1.0 / np.sqrt(fan_in)
        x = jax.random.normal(ks[0], (B, S, D), dtype=jnp.float32)
        gw1 = jax.random.uniform(ks[1], (D, D // 2), jnp.float32, -sd(D), sd(D))
        gb1 = jnp.zeros((D // 2,), jnp.float32)
        gw2 = jax.random.uniform(ks[2], (D // 2, E), jnp.float32, -sd(D // 2), sd(D // 2))
        gb2 = jnp.zeros((E,), jnp.float32)
        we1 = jax.random.uniform(ks[3], (E, D, H), jnp.float32, -sd(D), sd(D))
        be1 = jnp.zeros((E, H), jnp.float32)
        we2 = jax.random.uniform(ks[4], (E, H, D), jnp.float32, -sd(H), sd(H))
        be2 = jnp.zeros((E, D), jnp.float32)
        return {'x': x, 'gw1': gw1, 'gb1': gb1, 'gw2': gw2, 'gb2': gb2, 'we1': we1, 'be1': be1, 'we2': we2, 'be2': be2}
    _L0_ffn_all = _L0_ffn_setup()
    _L0_ffn_in = {k: v for k, v in _L0_ffn_all.items() if k in ('gw1', 'gb1', 'gw2', 'gb2', 'we1', 'be1', 'we2', 'be2')}
    del _L0_ffn_all
    return {'x': x, 'L0_tok_W': _L0_tok_in['W'], 'L0_tok_b': _L0_tok_in['b'], 'L0_tok_gamma': _L0_tok_in['gamma'], 'L0_tok_beta': _L0_tok_in['beta'], 'L0_attn_W_ih': _L0_attn_in['W_ih'], 'L0_attn_W_hh': _L0_attn_in['W_hh'], 'L0_attn_b_ih': _L0_attn_in['b_ih'], 'L0_attn_b_hh': _L0_attn_in['b_hh'], 'L0_ffn_gw1': _L0_ffn_in['gw1'], 'L0_ffn_gb1': _L0_ffn_in['gb1'], 'L0_ffn_gw2': _L0_ffn_in['gw2'], 'L0_ffn_gb2': _L0_ffn_in['gb2'], 'L0_ffn_we1': _L0_ffn_in['we1'], 'L0_ffn_be1': _L0_ffn_in['be1'], 'L0_ffn_we2': _L0_ffn_in['we2'], 'L0_ffn_be2': _L0_ffn_in['be2']}

def reference(x, L0_tok_W, L0_tok_b, L0_tok_gamma, L0_tok_beta, L0_attn_W_ih, L0_attn_W_hh, L0_attn_b_ih, L0_attn_b_hh, L0_ffn_gw1, L0_ffn_gb1, L0_ffn_gw2, L0_ffn_gb2, L0_ffn_we1, L0_ffn_be1, L0_ffn_we2, L0_ffn_be2):
    import jax
    import jax.numpy as jnp

    def _L0_tok_ref(x, W, b, gamma, beta):
        import jax, jax.numpy as jnp
        import numpy as np
        PATCH_LENGTH = 128
        PATCH_STRIDE = 64
        MODEL_DIM = 128
        LN_EPS = 0.001
        B, T, C = x.shape
        num_patches = (T - PATCH_LENGTH) // PATCH_STRIDE + 1
        idx = jnp.arange(num_patches)[:, None] * PATCH_STRIDE + jnp.arange(PATCH_LENGTH)[None, :]
        patches = x[:, idx, :]
        patches = patches.reshape(B, num_patches, PATCH_LENGTH * C)
        proj = jnp.einsum('bpf,fd->bpd', patches, W) + b
        mean = jnp.mean(proj, axis=-1, keepdims=True)
        var = jnp.mean(jnp.square(proj - mean), axis=-1, keepdims=True)
        out = (proj - mean) * jax.lax.rsqrt(var + LN_EPS) * gamma + beta
        return out

    def _L0_attn_ref(x, W_ih, W_hh, b_ih, b_hh):
        import jax, jax.numpy as jnp
        import numpy as np
        DIM = 128
        B, T = (32, 512)

        def _lstm(x, W_ih, W_hh, b_ih, b_hh):
            Bb, Tt, D = x.shape
            xg = jnp.einsum('btd,gd->btg', x, W_ih) + b_ih + b_hh
            xg = jnp.swapaxes(xg, 0, 1)

            def step(carry, xt):
                h, c = carry
                gates = xt + h @ W_hh.T
                i, f, g, o = jnp.split(gates, 4, axis=-1)
                i = jax.nn.sigmoid(i)
                f = jax.nn.sigmoid(f)
                g = jnp.tanh(g)
                o = jax.nn.sigmoid(o)
                c = f * c + i * g
                h = o * jnp.tanh(c)
                return ((h, c), h)
            h0 = jnp.zeros((Bb, D), dtype=x.dtype)
            (_, _), hs = jax.lax.scan(step, (h0, h0), xg)
            return jnp.swapaxes(hs, 0, 1)
        return _lstm(x, W_ih, W_hh, b_ih, b_hh)

    def _L0_ffn_ref(x, gw1, gb1, gw2, gb2, we1, be1, we2, be2):
        import jax, jax.numpy as jnp
        import numpy as np
        E = 8
        TOP_K = 2
        D = 128
        H = 256
        B, S = (16, 1024)
        b, s, d = x.shape
        xf = x.reshape(-1, d)
        T = xf.shape[0]
        gate_logits = jax.nn.relu(xf @ gw1 + gb1) @ gw2 + gb2
        gate_weights = jax.nn.softmax(gate_logits, axis=-1)
        top_w, top_idx = jax.lax.top_k(gate_weights, TOP_K)
        top_w = jax.nn.softmax(top_w, axis=-1)
        combine = jnp.zeros((T, E), dtype=xf.dtype)
        combine = combine.at[jnp.arange(T)[:, None], top_idx].add(top_w)
        out = jnp.zeros_like(xf)
        for e in range(E):
            h = jax.nn.gelu(xf @ we1[e] + be1[e], approximate=False)
            y = h @ we2[e] + be2[e]
            out = out + combine[:, e:e + 1] * y
        return out.reshape(b, s, d)
    h = _L0_tok_ref(x, L0_tok_W, L0_tok_b, L0_tok_gamma, L0_tok_beta)
    h = h + _L0_attn_ref(_layernorm(h, axis=-1), L0_attn_W_ih, L0_attn_W_hh, L0_attn_b_ih, L0_attn_b_hh)
    h = h + _L0_ffn_ref(_layernorm(h, axis=-1), L0_ffn_gw1, L0_ffn_gb1, L0_ffn_gw2, L0_ffn_gb2, L0_ffn_we1, L0_ffn_be1, L0_ffn_we2, L0_ffn_be2)
    return h

_drawn_inputs = setup_inputs


def setup_inputs(seed=0):
    import zlib

    import numpy as np

    out = dict(_drawn_inputs(seed))
    spreads = {'L0_tok_b': (0.0, 0.1),
     'L0_tok_gamma': (1.0, 0.2),
     'L0_tok_beta': (0.0, 0.1),
     'L0_ffn_gb1': (0.0, 0.1),
     'L0_ffn_gb2': (0.0, 0.1),
     'L0_ffn_be1': (0.0, 0.357),
     'L0_ffn_be2': (0.0, 0.1)}
    factors = {'L0_attn_b_ih': 2.683}
    for name, (base, spread) in spreads.items():
        noise = np.random.default_rng([zlib.crc32(name.encode()), seed]).standard_normal(out[name].shape)
        drawn = base * np.exp(spread * noise) if base else spread * noise
        out[name] = jnp.asarray(drawn.astype(out[name].dtype))
    for name, factor in factors.items():
        out[name] = (out[name] * factor).astype(out[name].dtype)
    return out
```

```python
from contextlib import ExitStack

import concourse.bass as bass
from concourse import mybir

F32 = mybir.dt.float32
U32 = mybir.dt.uint32
ALU = mybir.AluOpType
ACT = mybir.ActivationFunctionType
AX = mybir.AxisListType

P = 128
D = 128
B = 64
STRIDE = 128
PATCHES = 10
CHUNKS = PATCHES + 1
TILES = PATCHES * B // P
REST = TILES - 1
NE = 8
HC = 2
G4 = 4
TOK_EPS = 1e-3
LN_EPS = 1e-5
GH = 64

C_ID, C_BIAS, C_BE1, C_IOTA, C_GB1, C_GW1, C_GW2 = 0, 128, 136, 152, 160, 161, 225
C_COLS = 233
R_BE2, R_TOKB, R_LSTMB = 0, 128, 256
R_COLS = R_LSTMB + G4 * D

LOADS = ["x", "wtok", "rows", "gamma", "beta", "cols", "wih", "whh", "we1a", "we1b", "we2a", "we2b"]

PER_TILE = (
    [f"{n}{p}" for p in (0, 1) for n in (
        "rec_done", "pre_ready", "gates_ready", "fi_ready", "cell_ready", "tanhc_ready", "h_ready")]
    + ["hs_turned", "h_added", "ln_stats", "ln_mean", "ln_var", "ln_rstd", "xf_ready", "xf_turned", "xfT_ready"]
    + ["z_done", "z_ready", "logits_done", "lg_copied", "top_found", "top_index", "neg_max", "tanh_logits",
       "one_minus", "one_minus_inv", "exps", "exp_sum", "exp_sum_inv", "gap", "gap_tanh", "weight1", "weight2",
       "index_f", "part1", "part2", "comb", "comb_turned", "combT_ready", "bias_done", "acc_begun"]
    + [f"mm1_{e}" for e in range(NE)] + [f"gelu_{e}" for e in range(NE)]
    + [f"mm2_{e}" for e in range(NE)] + [f"acc_{e}" for e in range(NE)]
)


def audio_tower(nc, x, wtok, rows, gb, cols, wih, whh, we1, we2, out):
    with ExitStack() as ctx:
        def sb(name, shape, dt=F32):
            return ctx.enter_context(nc.sbuf_tensor(name, shape, dt))

        def bank(name):
            return ctx.enter_context(nc.psum_tensor(name, [P, 512], F32))

        def sem(name):
            return ctx.enter_context(nc.semaphore(name))

        xT = sb("xT", [P, CHUNKS * B])
        wtok_sb = sb("wtok_sb", [P, 2, D])
        rows_sb = sb("rows_sb", [NE, R_COLS])
        gamma = sb("gamma", [P, D])
        beta = sb("beta", [P, D])
        cols_sb = sb("cols_sb", [P, C_COLS])
        wih_sb = sb("wih_sb", [P, G4 * D])
        whh_sb = sb("whh_sb", [P, G4 * D])
        we1_sb = sb("we1_sb", [P, NE, HC, P])
        we2_sb = sb("we2_sb", [P, NE, HC, D])
        ones = sb("ones", [2, P])
        neg_half = sb("neg_half", [P, REST])
        bias_col = sb("bias_col", [P, G4])
        res = sb("res", [P, TILES, D])
        xhat = sb("xhat", [P, REST, D])
        xn = sb("xn", [P, TILES, D])
        xnT = sb("xnT", [P, TILES * P])
        bn = sb("bn", [P, REST, 6])
        mv = sb("mv", [P, REST, 2])
        ve = sb("ve", [P, REST])
        rstd = sb("rstd", [P, REST])
        nmr = sb("nmr", [P, REST])
        xg = sb("xg", [P, REST, 2, G4, B])
        cell = [sb(f"cell{p}", [P, 5, B]) for p in (0, 1)]
        pre = sb("pre", [P, G4, B])
        fi = sb("fi", [P, 2, B])
        tanhc = sb("tanhc", [P, B])
        h2 = sb("h2", [P, 2, B])
        lnbn = sb("lnbn", [P, 6])
        lnmv = sb("lnmv", [P, 2])
        lnve = sb("lnve", [P, 1])
        lnrs = sb("lnrs", [P, 1])
        xf = sb("xf", [P, D])
        xfT = sb("xfT", [P, P])
        zT = sb("zT", [GH + 1, P])
        lg = sb("lg", [P, 2 * NE])
        top_i = sb("top_i", [P, NE], U32)
        top_f = sb("top_f", [P, 2])
        nmax = sb("nmax", [P, 1])
        th = sb("th", [P, 2 * NE])
        den = sb("den", [P, 2 * NE])
        rden = sb("rden", [P, 2 * NE])
        ex = sb("ex", [P, 2 * NE])
        esum = sb("esum", [P, 1])
        rsum = sb("rsum", [P, 1])
        ngap = sb("ngap", [P, 1])
        tgap = sb("tgap", [P, 1])
        tw1 = sb("tw1", [P, 1])
        tw2 = sb("tw2", [P, 1])
        cp1 = sb("cp1", [P, NE])
        cp2 = sb("cp2", [P, NE])
        comb = sb("comb", [P, NE])
        combT = sb("combT", [NE, P])
        hidT = [sb(f"hidT{k}", [P, HC, P]) for k in range(4)]

        hid_ps = [bank("hid0"), bank("hid1")]
        y_ps = [bank("y0"), bank("y1")]
        gate_ps = bank("gate_ps")
        turn_ps = bank("turn_ps")
        lg_ps = bank("lg_ps")
        cb_ps = bank("cb_ps")

        load = {n: sem(f"load_{n}") for n in LOADS}
        S = {n: sem(n) for n in PER_TILE}
        pool_ready = sem("pool_ready")
        scaled = sem("scaled")
        bias_scaled = sem("bias_scaled")
        tok_done = sem("tok_done")
        front = sem("front")
        front_rstd = sem("front_rstd")
        front_act = sem("front_act")
        xn_turned = sem("xn_turned")
        xnT_ready = sem("xnT_ready")
        first_pre = sem("first_pre")
        xg_done = sem("xg_done")
        xg_ready = sem("xg_ready")
        stored = sem("stored")

        ident = cols_sb[:, C_ID:C_ID + P]
        iota = cols_sb[:, C_IOTA:C_IOTA + NE]

        def gate_bank(p):
            return gate_ps[:, p * G4 * B:(p + 1) * G4 * B].rearrange("q (g b) -> q g b", g=G4)

        block = ctx.enter_context(nc.Block())

        @block.sync
        def _(sp):
            sp.dma_start(xT[:], x).then_inc(load["x"], 16)
            sp.dma_start(cols_sb[:], cols).then_inc(load["cols"], 16)
            sp.dma_start(gamma[:], gb[0:1, :].broadcast_to([P, D])).then_inc(load["gamma"], 16)
            sp.dma_start(whh_sb[:], whh).then_inc(load["whh"], 16)
            h = NE // 2
            sp.dma_start(we1_sb[:, 0:h], we1[:, 0:h]).then_inc(load["we1a"], 16)
            sp.dma_start(we1_sb[:, h:NE], we1[:, h:NE]).then_inc(load["we1b"], 16)
            for t in range(TILES):
                sp.wait_ge(S[f"acc_{NE - 1}"], t + 1)
                for p in (0, 1):
                    sp.dma_start(out[:, 2 * t + p, :], res[p * B:(p + 1) * B, t, :]).then_inc(stored, 16)
            sp.wait_ge(stored, 16 * PATCHES)

        @block.gpsimd
        def _(pool):
            nc.gpsimd.memset(ones[:], 1.0).then_inc(pool_ready, 1)
            nc.gpsimd.memset(neg_half[:], -0.5).then_inc(pool_ready, 1)
            nc.gpsimd.memset(cell[0][:, 0, :], 0.0).then_inc(pool_ready, 1)
            pool.wait_ge(pool_ready, 3)
            nc.gpsimd.memset(zT[GH:GH + 1, :], 1.0).then_inc(pool_ready, 1)
            pool.wait_ge(pool_ready, 4)
            for n, (a, need) in enumerate(((1, FRONT_VE[0]), (1, FRONT_VE[1]), (REST, FRONT_VE[2]), (REST, FRONT_VE[3]))):
                pool.wait_ge(front, need)
                nc.gpsimd.tensor_tensor(rstd[:, 0:a], ve[:, 0:a], neg_half[:, 0:a], ALU.pow).then_inc(front_rstd, 1)
            for t in range(TILES):
                pool.wait_ge(S["ln_var"], t + 1)
                nc.gpsimd.tensor_tensor(lnrs[:], lnve[:], neg_half[:, 0:1], ALU.pow).then_inc(S["ln_rstd"], 1)

        @block.tensor
        def _(pe):
            def project(dst, t):
                pe.matmul(dst, ones[0:1, :], rows_sb[0:1, R_TOKB:R_TOKB + D], start=True, stop=False)
                for k in (0, 1):
                    mm = pe.matmul(dst, xT[:, (2 * t + k) * B:(2 * t + k + 2) * B], wtok_sb[:, k, :],
                                   start=False, stop=k == 1)
                return mm

            def recur(t, p, dst, start):
                for g in range(G4):
                    mm = pe.matmul(dst[:, g, :], whh_sb[:, g * D:(g + 1) * D], h2[:, 1 - p, :],
                                   start=start, stop=True, skip_group_check=True)
                mm.then_inc(S[f"rec_done{p}"], 1)

            def turn_h(t):
                pe.wait_ge(S["h_ready1"], t + 1)
                if t >= 1:
                    pe.wait_ge(S["xfT_ready"], t)
                pe.transpose(turn_ps[:, 0:P], h2[:].rearrange("q s b -> q (s b)"), ident).then_inc(S["hs_turned"], 1)

            def turn_xf(t):
                pe.wait_ge(S["xf_ready"], t + 1)
                pe.transpose(turn_ps[:, P:2 * P], xf[:], ident).then_inc(S["xf_turned"], 1)

            def gate_hidden(t):
                pe.wait_ge(S["xfT_ready"], t + 1)
                if t >= 1:
                    pe.wait_ge(S["lg_copied"], t)
                pe.matmul(lg_ps[0:GH, 0:P], cols_sb[:, C_GW1:C_GW1 + GH], xfT[:], start=True, stop=True
                          ).then_inc(S["z_done"], 1)

            def gate_logits(t):
                pe.wait_ge(S["z_ready"], t + 1)
                pe.matmul(lg_ps[:, P:P + NE], zT[:], cols_sb[0:GH + 1, C_GW2:C_GW2 + NE], start=True, stop=True
                          ).then_inc(S["logits_done"], 1)

            def turn_comb(t):
                pe.wait_ge(S["comb"], t + 1)
                if t >= 1:
                    pe.wait_ge(S["acc_begun"], t)
                pe.transpose(cb_ps[0:NE, 0:P], comb[:], ident).then_inc(S["comb_turned"], 1)

            def expert_bias(t):
                pe.wait_ge(S["combT_ready"], t + 1)
                pe.matmul(cb_ps[:, P:2 * P], combT[:], rows_sb[:, R_BE2:R_BE2 + D], start=True, stop=True
                          ).then_inc(S["bias_done"], 1)

            def mm1(t, e):
                if e >= 2:
                    pe.wait_ge(S[f"gelu_{e - 2}"], t + 1)
                elif t >= 1:
                    pe.wait_ge(S[f"gelu_{NE - 2 + e}"], t)
                for j in range(HC):
                    mm = pe.matmul(hid_ps[e % 2][:, j * P:(j + 1) * P], we1_sb[:, e, j, :], xfT[:],
                                   start=True, stop=True)
                mm.then_inc(S[f"mm1_{e}"], 1)

            def mm2(t, e):
                pe.wait_ge(S[f"gelu_{e}"], t + 1)
                if t >= 1 and e % 4 == 0:
                    pe.wait_ge(S[f"acc_{e + 3}"], t)
                for j in range(HC):
                    mm = pe.matmul(y_ps[e // 4][:, (e % 4) * D:(e % 4 + 1) * D], hidT[e % 4][:, j, :],
                                   we2_sb[:, e, j, :], start=j == 0, stop=j == 1)
                mm.then_inc(S[f"mm2_{e}"], 1)

            pe.wait_ge(load["rows"], 16)
            pe.wait_ge(load["wtok"], 16)
            pe.wait_ge(load["x"], 16)
            pe.wait_ge(pool_ready, 1)
            project(cb_ps[:, 0:D], 0).then_inc(tok_done, 1)
            for t in range(1, TILES):
                mm = project(y_ps[0][:, (t - 1) * D:t * D], t)
            mm.then_inc(tok_done, 1)

            def first_gate(g):
                return gate_ps[:].rearrange("q (s g b) -> q g s b", s=2, g=G4)[:, g]

            pe.wait_ge(bias_scaled, 1)
            for g in range(G4):
                pe.matmul(first_gate(g), rows_sb[0:2, R_LSTMB + g * D:R_LSTMB + (g + 1) * D], ones[:],
                          start=g == 0, stop=False, skip_group_check=True)
            pe.wait_ge(load["cols"], 16)
            pe.wait_ge(front, FRONT_XN0)
            pe.transpose(turn_ps[:, 0:P], xn[:, 0, :], ident).then_inc(xn_turned, 1)
            pe.wait_ge(scaled, 1)
            pe.wait_ge(xnT_ready, 1)
            for g in range(G4):
                mm = pe.matmul(first_gate(g), wih_sb[:, g * D:(g + 1) * D], xnT[:, 0:P],
                               start=False, stop=True, skip_group_check=True)
            mm.then_inc(first_pre, 1)

            pe.wait_ge(scaled, 2)
            pe.wait_ge(S["h_ready0"], 1)
            recur(0, 1, gate_bank(1), False)

            pe.wait_ge(front, FRONT_XN)
            for t in range(1, TILES):
                mm = pe.transpose(y_ps[1][:, (t - 1) * P:t * P], xn[:, t, :], ident)
            mm.then_inc(xn_turned, 1)
            pe.wait_ge(xnT_ready, 2)
            for g, dst in enumerate((hid_ps[0], hid_ps[1], lg_ps, cb_ps)):
                pe.matmul(dst[:], wih_sb[:, g * D:(g + 1) * D], xnT[:, P:TILES * P],
                          start=True, stop=True).then_inc(xg_done, 1)
            turn_h(0)
            turn_xf(0)
            pe.wait_ge(xg_ready, G4)
            pe.wait_ge(load["we1a"], 16)
            pe.wait_ge(load["we2a"], 16)
            pe.wait_ge(load["we1b"], 16)
            pe.wait_ge(load["we2b"], 16)

            def step(t, p):
                pe.wait_ge(S[f"h_ready{1 - p}"], t + p)
                recur(t, p, gate_bank(0), True)

            def tile(t, lstm):
                gate_hidden(t)
                mm1(t, 0)
                if lstm:
                    step(t + 1, 0)
                gate_logits(t)
                mm1(t, 1)
                mm2(t, 0)
                mm1(t, 2)
                mm2(t, 1)
                if lstm:
                    step(t + 1, 1)
                mm1(t, 3)
                mm2(t, 2)
                mm1(t, 4)
                turn_comb(t)
                mm2(t, 3)
                mm1(t, 5)
                expert_bias(t)
                mm2(t, 4)
                if lstm:
                    turn_h(t + 1)
                mm1(t, 6)
                mm2(t, 5)
                mm1(t, 7)
                mm2(t, 6)
                mm2(t, 7)
                if lstm:
                    turn_xf(t + 1)

            for t in range(TILES - 1):
                tile(t, True)
            tile(TILES - 1, False)

        @block.scalar
        def _(act):
            act.dma_start(wtok_sb[:], wtok).then_inc(load["wtok"], 16)
            act.dma_start(rows_sb[:], rows).then_inc(load["rows"], 16)
            act.dma_start(beta[:], gb[1:2, :].broadcast_to([P, D])).then_inc(load["beta"], 16)
            act.dma_start(wih_sb[:], wih).then_inc(load["wih"], 16)
            h = NE // 2
            act.dma_start(we2_sb[:, 0:h], we2[:, 0:h]).then_inc(load["we2a"], 16)
            act.dma_start(we2_sb[:, h:NE], we2[:, h:NE]).then_inc(load["we2b"], 16)

            act.wait_ge(load["rows"], 16)
            nc.scalar.mul(rows_sb[0:2, R_LSTMB + D:], rows_sb[0:2, R_LSTMB + D:], 0.5).then_inc(bias_scaled, 1)
            act.wait_ge(load["wih"], 16)
            nc.scalar.mul(wih_sb[:, D:], wih_sb[:, D:], 0.5).then_inc(scaled, 1)
            act.wait_ge(load["whh"], 16)
            nc.scalar.mul(whh_sb[:, 0:D], whh_sb[:, 0:D], 0.5)
            nc.scalar.mul(whh_sb[:, D:], whh_sb[:, D:], 0.25).then_inc(scaled, 1)

            act.wait_ge(xn_turned, 1)
            nc.scalar.copy(xnT[:, 0:P], turn_ps[:, 0:P]).then_inc(xnT_ready, 1)

            def gates(t, p, src, ready, n):
                act.wait_ge(ready, n)
                if t >= 1 or p == 1:
                    act.wait_ge(S[f"h_ready{1 - p}"], t + p)
                nc.scalar.activation(cell[p][:, 1:5, :], src, ACT.Tanh).then_inc(S[f"gates_ready{p}"], 1)

            def tanh_cell(t, p):
                act.wait_ge(S[f"cell_ready{p}"], t + 1)
                nc.scalar.activation(tanhc[:], cell[1 - p][:, 0, :], ACT.Tanh, scale=0.5
                                     ).then_inc(S[f"tanhc_ready{p}"], 1)

            gates(0, 0, gate_bank(0), first_pre, 1)
            tanh_cell(0, 0)
            gates(0, 1, gate_bank(1), S["rec_done1"], 1)
            act.wait_ge(front, FRONT_NMR)
            for t in range(REST):
                a = nc.scalar.activation(xhat[:, t, :], y_ps[0][:, t * D:(t + 1) * D], ACT.Identity,
                                         bias=nmr[:, t:t + 1], scale=rstd[:, t:t + 1])
            a.then_inc(front_act, 1)
            tanh_cell(0, 1)
            act.wait_ge(xn_turned, 2)
            nc.scalar.copy(xnT[:, P:], y_ps[1][:]).then_inc(xnT_ready, 1)
            act.wait_ge(front, FRONT_BIAS)
            for g, src in enumerate((hid_ps[0], hid_ps[1], lg_ps, cb_ps)):
                act.wait_ge(xg_done, g + 1)
                nc.scalar.activation(xg[:, :, :, g, :], src[:].rearrange("q (t s b) -> q t s b", t=REST, s=2),
                                     ACT.Identity, bias=bias_col[:, g:g + 1]).then_inc(xg_ready, 1)

            def xfT_copy(t):
                act.wait_ge(S["xf_turned"], t + 1)
                if t >= 1:
                    act.wait_ge(S[f"mm1_{NE - 1}"], t)
                nc.scalar.copy(xfT[:], turn_ps[:, P:2 * P]).then_inc(S["xfT_ready"], 1)

            def gelu(t, e):
                act.wait_ge(S[f"mm1_{e}"], t + 1)
                if e >= 4:
                    act.wait_ge(S[f"mm2_{e - 4}"], t + 1)
                elif t >= 1:
                    act.wait_ge(S[f"mm2_{e + 4}"], t)
                for j in range(HC):
                    c = C_BE1 + HC * e + j
                    a = nc.scalar.activation(hidT[e % 4][:, j, :], hid_ps[e % 2][:, j * P:(j + 1) * P], ACT.Gelu,
                                             bias=cols_sb[:, c:c + 1])
                a.then_inc(S[f"gelu_{e}"], 1)

            def z(t):
                act.wait_ge(S["z_done"], t + 1)
                if t >= 1:
                    act.wait_ge(S["logits_done"], t)
                nc.scalar.activation(zT[0:GH, :], lg_ps[0:GH, 0:P], ACT.Relu, bias=cols_sb[0:GH, C_GB1:C_GB1 + 1]
                                     ).then_inc(S["z_ready"], 1)

            def tanh_logits(t):
                act.wait_ge(S["neg_max"], t + 1)
                nc.scalar.activation(th[:], lg[:], ACT.Tanh, bias=nmax[:], scale=0.5).then_inc(S["tanh_logits"], 1)

            def tanh_gap(t):
                act.wait_ge(S["gap"], t + 1)
                nc.scalar.activation(tgap[:], ngap[:], ACT.Tanh, scale=-0.5).then_inc(S["gap_tanh"], 1)

            def combT_copy(t):
                act.wait_ge(S["comb_turned"], t + 1)
                if t >= 1:
                    act.wait_ge(S["bias_done"], t)
                nc.scalar.copy(combT[:], cb_ps[0:NE, 0:P]).then_inc(S["combT_ready"], 1)

            def tile(t, lstm):
                z(t)
                gelu(t, 0)
                if lstm:
                    gates(t + 1, 0, pre[:], S["pre_ready0"], t + 1)
                gelu(t, 1)
                if lstm:
                    tanh_cell(t + 1, 0)
                tanh_logits(t)
                gelu(t, 2)
                tanh_gap(t)
                if lstm:
                    gates(t + 1, 1, pre[:], S["pre_ready1"], t + 1)
                gelu(t, 3)
                if lstm:
                    tanh_cell(t + 1, 1)
                gelu(t, 4)
                combT_copy(t)
                gelu(t, 5)
                gelu(t, 6)
                gelu(t, 7)
                if lstm:
                    xfT_copy(t + 1)

            xfT_copy(0)
            for t in range(TILES - 1):
                tile(t, True)
            tile(TILES - 1, False)

        @block.vector
        def _(dve):
            n_front = [0]

            def link(ins):
                n_front[0] += 1
                ins.then_inc(front, 1)
                dve.wait_ge(front, n_front[0])

            def step(ins, name, t):
                ins.then_inc(S[name], 1)
                dve.wait_ge(S[name], t + 1)

            def front_stats(srcs, n, eps, rstd_n):
                for k, src in enumerate(srcs):
                    last = nc.vector.bn_stats(bn[:, k, :], src)
                link(last)
                for k in range(n):
                    last = nc.vector.bn_aggr(mv[:, k, :], bn[:, k, :])
                link(last)
                link(nc.vector.tensor_scalar(ve[:, 0:n], mv[:, 0:n, 1], eps, None, ALU.add))
                mark = n_front[0]
                dve.wait_ge(front_rstd, rstd_n)
                return mark

            dve.wait_ge(tok_done, 1)
            m0 = front_stats([cb_ps[:, 0:D]], 1, TOK_EPS, 1)
            link(nc.vector.tensor_scalar(res[:, 0, :], cb_ps[:, 0:D], mv[:, 0, 0:1], rstd[:, 0:1],
                                         ALU.subtract, ALU.mult))
            dve.wait_ge(load["gamma"], 16)
            link(nc.vector.tensor_tensor(res[:, 0, :], res[:, 0, :], gamma[:], ALU.mult))
            dve.wait_ge(load["beta"], 16)
            link(nc.vector.tensor_tensor(res[:, 0, :], res[:, 0, :], beta[:], ALU.add))
            m1 = front_stats([res[:, 0, :]], 1, LN_EPS, 2)
            link(nc.vector.tensor_scalar(xn[:, 0, :], res[:, 0, :], mv[:, 0, 0:1], rstd[:, 0:1],
                                         ALU.subtract, ALU.mult))
            xn0 = n_front[0]

            dve.wait_ge(tok_done, 2)
            m2 = front_stats([y_ps[0][:, t * D:(t + 1) * D] for t in range(REST)], REST, TOK_EPS, 3)
            link(nc.vector.scalar_tensor_tensor(nmr[:], mv[:, :, 0], -1.0, rstd[:], ALU.mult, ALU.mult))
            mnmr = n_front[0]

            def cell_update(t, p):
                dve.wait_ge(S[f"gates_ready{p}"], t + 1)
                step(nc.vector.scalar_tensor_tensor(fi[:], cell[p][:, 2:4, :], 1.0, cell[p][:, 0:2, :],
                                                    ALU.add, ALU.mult), f"fi_ready{p}", t)
                nc.vector.scalar_tensor_tensor(cell[1 - p][:, 0, :], fi[:, 0, :], 0.5, fi[:, 1, :],
                                               ALU.mult, ALU.add).then_inc(S[f"cell_ready{p}"], 1)

            def hidden(t, p):
                dve.wait_ge(S[f"tanhc_ready{p}"], t + 1)
                if t >= 1:
                    dve.wait_ge(S["hs_turned"], t)
                nc.vector.scalar_tensor_tensor(h2[:, p, :], cell[p][:, 4, :], 1.0, tanhc[:], ALU.add, ALU.mult
                                               ).then_inc(S[f"h_ready{p}"], 1)

            def add_pre(t, p):
                dve.wait_ge(S[f"rec_done{p}"], t if p == 0 else t + 1)
                nc.vector.tensor_tensor(pre[:], gate_bank(0), xg[:, t - 1, p], ALU.add
                                        ).then_inc(S[f"pre_ready{p}"], 1)

            dve.wait_ge(pool_ready, 4)
            cell_update(0, 0)
            hidden(0, 0)
            dve.wait_ge(load["cols"], 16)
            link(nc.vector.tensor_tensor(bias_col[:], cols_sb[:, C_BIAS:C_BIAS + G4],
                                         cols_sb[:, C_BIAS + G4:C_BIAS + 2 * G4], ALU.add))
            link(nc.vector.tensor_scalar(bias_col[:, 1:], bias_col[:, 1:], 0.5, None, ALU.mult))
            mbias = n_front[0]
            cell_update(0, 1)
            dve.wait_ge(front_act, 1)
            link(nc.vector.tensor_tensor(xhat[:], xhat[:], gamma[:].unsqueeze(1).broadcast_to([P, REST, D]), ALU.mult))
            hidden(0, 1)
            link(nc.vector.tensor_tensor(res[:, 1:, :], xhat[:], beta[:].unsqueeze(1).broadcast_to([P, REST, D]), ALU.add))
            m3 = front_stats([res[:, t, :] for t in range(1, TILES)], REST, LN_EPS, 4)
            for t in range(1, TILES):
                last = nc.vector.tensor_scalar(xn[:, t, :], res[:, t, :], mv[:, t - 1, 0:1], rstd[:, t - 1:t],
                                               ALU.subtract, ALU.mult)
            link(last)
            xn1 = n_front[0]
            assert ([m0, m1, m2, m3], xn0, xn1, mnmr, mbias) == (
                FRONT_VE, FRONT_XN0, FRONT_XN, FRONT_NMR, FRONT_BIAS), ([m0, m1, m2, m3], xn0, xn1, mnmr, mbias)

            def ln_first(t):
                dve.wait_ge(S["hs_turned"], t + 1)
                step(nc.vector.scalar_tensor_tensor(res[:, t, :], turn_ps[:, 0:P], 0.5, res[:, t, :],
                                                    ALU.mult, ALU.add), "h_added", t)
                step(nc.vector.bn_stats(lnbn[:], res[:, t, :]), "ln_stats", t)
                step(nc.vector.bn_aggr(lnmv[:], lnbn[:]), "ln_mean", t)
                nc.vector.tensor_scalar(lnve[:], lnmv[:, 1:2], LN_EPS, None, ALU.add).then_inc(S["ln_var"], 1)

            def ln_last(t):
                dve.wait_ge(S["ln_rstd"], t + 1)
                if t >= 1:
                    dve.wait_ge(S["xf_turned"], t)
                nc.vector.tensor_scalar(xf[:], res[:, t, :], lnmv[:, 0:1], lnrs[:], ALU.subtract, ALU.mult
                                        ).then_inc(S["xf_ready"], 1)

            def top_two(t):
                dve.wait_ge(S["logits_done"], t + 1)
                step(nc.vector.tensor_copy(lg[:, 0:NE], lg_ps[:, P:P + NE]), "lg_copied", t)
                step(nc.vector.max(lg[:, NE:], lg[:, 0:NE]), "top_found", t)
                nc.vector.tensor_scalar(nmax[:], lg[:, NE:NE + 1], -0.5, None, ALU.mult).then_inc(S["neg_max"], 1)
                step(nc.vector.max_index(top_i[:], lg[:, NE:], lg[:, 0:NE]), "top_index", t)
                step(nc.vector.tensor_copy(top_f[:], top_i[:, 0:2]), "index_f", t)

            def softmax_gap(t):
                dve.wait_ge(S["tanh_logits"], t + 1)
                step(nc.vector.tensor_scalar(den[:], th[:], -1.0, 1.0, ALU.mult, ALU.add), "one_minus", t)
                step(nc.vector.reciprocal(rden[:], den[:]), "one_minus_inv", t)
                step(nc.vector.scalar_tensor_tensor(ex[:], th[:], 1.0, rden[:], ALU.add, ALU.mult), "exps", t)
                step(nc.vector.tensor_reduce(esum[:], ex[:, 0:NE], AX.X, ALU.add), "exp_sum", t)
                step(nc.vector.reciprocal(rsum[:], esum[:]), "exp_sum_inv", t)
                nc.vector.scalar_tensor_tensor(ngap[:], ex[:, NE + 1:NE + 2], -1.0, rsum[:], ALU.add, ALU.mult
                                               ).then_inc(S["gap"], 1)

            def combine_weights(t):
                dve.wait_ge(S["gap_tanh"], t + 1)
                nc.vector.tensor_scalar(tw1[:], tgap[:], 0.5, 0.5, ALU.mult, ALU.add).then_inc(S["weight1"], 1)
                step(nc.vector.tensor_scalar(tw2[:], tgap[:], -0.5, 0.5, ALU.mult, ALU.add), "weight2", t)
                dve.wait_ge(S["weight1"], t + 1)
                nc.vector.tensor_scalar(cp1[:], iota, top_f[:, 0:1], tw1[:], ALU.is_equal, ALU.mult
                                        ).then_inc(S["part1"], 1)
                step(nc.vector.tensor_scalar(cp2[:], iota, top_f[:, 1:2], tw2[:], ALU.is_equal, ALU.mult),
                     "part2", t)
                dve.wait_ge(S["part1"], t + 1)
                step(nc.vector.tensor_tensor(comb[:], cp1[:], cp2[:], ALU.add), "comb", t)

            def acc_begin(t):
                dve.wait_ge(S["bias_done"], t + 1)
                step(nc.vector.tensor_tensor(res[:, t, :], res[:, t, :], cb_ps[:, P:2 * P], ALU.add),
                     "acc_begun", t)

            def accumulate(t, b):
                dve.wait_ge(S[f"mm2_{4 * b + 3}"], t + 1)
                for e in range(4 * b, 4 * b + 4):
                    step(nc.vector.scalar_tensor_tensor(res[:, t, :], y_ps[b][:, (e % 4) * D:(e % 4 + 1) * D],
                                                        comb[:, e:e + 1], res[:, t, :], ALU.mult, ALU.add),
                         f"acc_{e}", t)

            def tile(t, lstm):
                if lstm:
                    add_pre(t + 1, 0)
                    cell_update(t + 1, 0)
                top_two(t)
                if lstm:
                    hidden(t + 1, 0)
                softmax_gap(t)
                if lstm:
                    add_pre(t + 1, 1)
                    combine_weights(t)
                    cell_update(t + 1, 1)
                    hidden(t + 1, 1)
                else:
                    combine_weights(t)
                acc_begin(t)
                accumulate(t, 0)
                if lstm:
                    ln_first(t + 1)
                    ln_last(t + 1)
                accumulate(t, 1)

            ln_first(0)
            ln_last(0)
            for t in range(TILES - 1):
                tile(t, True)
            tile(TILES - 1, False)


FRONT_VE = [3, 9, 13, 21]
FRONT_XN0, FRONT_XN, FRONT_NMR, FRONT_BIAS = 10, 22, 14, 16


def kernel(x, L0_tok_W, L0_tok_b, L0_tok_gamma, L0_tok_beta, L0_attn_W_ih, L0_attn_W_hh, L0_attn_b_ih,
           L0_attn_b_hh, L0_ffn_gw1, L0_ffn_gb1, L0_ffn_gw2, L0_ffn_gb2, L0_ffn_we1, L0_ffn_be1, L0_ffn_we2,
           L0_ffn_be2):
    import numpy as np
    import concourse.bacc as bacc
    from concourse.bass_utils import run_bass_kernel_spmd

    f = np.float32
    order = (2, 1, 0, 3)

    def by_gate(a):
        return np.concatenate([np.asarray(a).reshape(4, D, -1)[g] for g in order], axis=0)

    xs = np.asarray(x).reshape(B, -1)[:, :CHUNKS * STRIDE].reshape(B, CHUNKS, STRIDE).transpose(2, 1, 0)
    b_ih, b_hh = by_gate(L0_attn_b_ih).reshape(4, D), by_gate(L0_attn_b_hh).reshape(4, D)
    cols = np.zeros((P, C_COLS), f)
    cols[:, C_ID:C_ID + P] = np.eye(P, dtype=f)
    cols[:, C_BIAS:C_BIAS + 4] = b_ih.T
    cols[:, C_BIAS + 4:C_BIAS + 8] = b_hh.T
    cols[:, C_BE1:C_BE1 + NE * HC] = np.asarray(L0_ffn_be1).reshape(NE * HC, P).T
    cols[:, C_IOTA:C_IOTA + NE] = np.arange(NE, dtype=f)
    cols[:GH, C_GB1] = np.asarray(L0_ffn_gb1)
    cols[:, C_GW1:C_GW1 + GH] = np.asarray(L0_ffn_gw1)
    cols[:GH, C_GW2:C_GW2 + NE] = np.asarray(L0_ffn_gw2)
    cols[GH, C_GW2:C_GW2 + NE] = np.asarray(L0_ffn_gb2)
    rows = np.zeros((NE, R_COLS), f)
    rows[:, R_BE2:R_BE2 + D] = np.asarray(L0_ffn_be2)
    rows[0, R_TOKB:R_TOKB + D] = np.asarray(L0_tok_b)
    rows[0, R_LSTMB:] = b_ih.reshape(-1)
    rows[1, R_LSTMB:] = b_hh.reshape(-1)
    arrays = {
        "x": xs.reshape(P, CHUNKS * B),
        "wtok": np.asarray(L0_tok_W).reshape(2, P, D).transpose(1, 0, 2),
        "rows": rows,
        "gb": np.stack([np.asarray(L0_tok_gamma), np.asarray(L0_tok_beta)]),
        "cols": cols,
        "wih": by_gate(L0_attn_W_ih).T,
        "whh": by_gate(L0_attn_W_hh).T,
        "we1": np.asarray(L0_ffn_we1).reshape(NE, D, HC, P).transpose(1, 0, 2, 3),
        "we2": np.asarray(L0_ffn_we2).reshape(NE, HC, P, D).transpose(2, 0, 1, 3),
    }
    arrays = {n: np.ascontiguousarray(a) for n, a in arrays.items()}
    nc = bacc.Bacc("TRN2", target_bir_lowering=False, num_devices=1)
    args = [nc.dram_tensor(n, a.shape, F32, kind="ExternalInput").ap() for n, a in arrays.items()]
    out = nc.dram_tensor("out", (B, PATCHES, D), F32, kind="ExternalOutput").ap()
    audio_tower(nc, *args, out)
    got = run_bass_kernel_spmd(nc, [arrays], core_ids=[0])
    return got.results[0]["out"]
```

```python
from contextlib import ExitStack

import concourse.bass as bass
from concourse import mybir

F32 = mybir.dt.float32
F16 = mybir.dt.float16
U32 = mybir.dt.uint32
ALU = mybir.AluOpType
ACT = mybir.ActivationFunctionType
AX = mybir.AxisListType

P = 128
D = 128
B = 64
STRIDE = 128
PATCHES = 10
CHUNKS = PATCHES + 1
TILES = PATCHES * B // P
NE = 8
HC = 2
G4 = 4
TOK_EPS = 1e-3
LN_EPS = 1e-5
GH = 64
W1 = GH + NE * HC * P
PARTS = 4
PART_ENDS = [0] + [GH + (k + 1) * (W1 - GH) // PARTS for k in range(PARTS)]
HALF1 = PART_ENDS[PARTS // 2]

A_X, A_W = 0, 3 * B
A_COLS = A_W + 2 * D
C_ID, C_BE1, C_IOTA, C_GB1, C_GW2, C_BIH, C_BHH, C_WIH = 0, 128, 144, 152, 153, 161, 165, 169
C_COLS = C_WIH + G4 * D
X_WHH = (CHUNKS - 3) * B
X_COLS = X_WHH + G4 * D
R_BE2, R_TOKB, R_LSTMB = 0, 128, 256
R_COLS = R_LSTMB + G4 * D

EXP1 = float(1 << 23)
HH_TO, HH_BACK = 203 * EXP1, 51 * EXP1
W1_UP = 6
W1_FROM, W1_MOST = 77.0 - W1_UP, 12.0
W1_BACK = 2.0 ** -W1_UP

LOADS = ["first", "rows", "affine", "cols", "xrest", "we1a", "we1b", "we2a", "we2b"]

FRONT = (
    ["ones", "neg_half", "cell_zero", "z_one", "bias_sum", "bias_half"]
    + ["norm_hh"]
    + ["table", "bias_scaled", "wih_scaled", "sq_hh", "sq_w1", "hh_hi", "w1_hi"]
    + ["idle", "hh_v", "hh_scale", "hh_lo", "w1_sum", "w1_v", "w1_k", "w1_exp", "w1_scale", "w1_lo"]
)

PER_TILE = (
    ["proj", "stats_a", "mean_a", "ve_a", "rstd_a", "centred", "res", "stats_b", "mean_b", "ve_b", "rstd_b",
     "xn", "turned", "xnT", "pre", "xg", "biased"]
    + [f"{n}{p}" for p in (0, 1) for n in (
        "rec_done", "pre_ready", "gates_ready", "fi_ready", "cell_ready", "tanhc_ready", "h_hi", "h_ready", "h_lo")]
    + ["hs_turned", "h_added", "ln_stats", "ln_mean", "ln_var", "ln_rstd", "xf_ready", "xf_turned", "xf_hi", "xf_lo"]
    + ["z_done", "z_ready", "logits_done", "top_found", "top_index", "neg_max", "tanh_logits",
       "one_minus", "one_minus_inv", "exps", "exp_sum", "exp_sum_inv", "gap", "gap_tanh", "weight1", "weight2",
       "index_f", "part1", "part2", "comb", "comb_turned", "combT_ready", "bias_done", "bias_added"]
    + [f"mm1_{e}" for e in range(NE)] + [f"gelu_{e}" for e in range(NE)]
    + [f"mm2_{e}" for e in range(NE)] + [f"acc_{e}" for e in range(NE)]
)


def audio_tower(nc, first, rows, affine, cols, xrest, we1, we2, out):
    with ExitStack() as ctx:
        def sb(name, shape, dt=F32):
            return ctx.enter_context(nc.sbuf_tensor(name, shape, dt))

        def bank(name):
            return ctx.enter_context(nc.psum_tensor(name, [P, 512], F32))

        def sem(name):
            return ctx.enter_context(nc.semaphore(name))

        first_sb = sb("first_sb", [P, A_COLS])
        xrest_sb = sb("xrest_sb", [P, X_COLS])
        rows_sb = sb("rows_sb", [NE, R_COLS])
        affine_sb = sb("affine_sb", [P, 2, D])
        cols_sb = sb("cols_sb", [P, C_COLS])
        we1_sb = sb("we1_sb", [P, W1])
        we2_sb = sb("we2_sb", [P, NE, HC, D])
        whh_hi = sb("whh_hi", [P, G4 * D], F16)
        whh_lo = sb("whh_lo", [P, G4 * D], F16)
        we1_hi = sb("we1_hi", [P, W1], F16)
        we1_lo = sb("we1_lo", [P, W1], F16)
        ones = sb("ones", [P, P])
        idle = sb("idle", [P, P], F16)
        neg_half = sb("neg_half", [P, 1])
        squares = sb("squares", [P, W1], F16)
        sumsq_hh = sb("sumsq_hh", [P, 1])
        sumsq_w1 = sb("sumsq_w1", [P, 3])
        v_hh = sb("v_hh", [P, 1], U32)
        v_w1 = sb("v_w1", [P, 3], U32)
        scale_hh = sb("scale_hh", [P, 3], U32)
        scale_w1 = sb("scale_w1", [P, 2], U32)
        res = sb("res", [P, TILES, D])
        centred = sb("centred", [P, TILES, D])
        xn = sb("xn", [P, TILES, D])
        xnT = sb("xnT", [P, TILES, P])
        bn = sb("bn", [P, TILES, 6])
        mv = sb("mv", [P, TILES, 2])
        ve = sb("ve", [P, TILES])
        rstd = sb("rstd", [P, TILES])
        xg = sb("xg", [P, TILES, 2, G4, B])
        bias = sb("bias", [P, G4])
        cell = [sb(f"cell{p}", [P, 5, B]) for p in (0, 1)]
        pre = sb("pre", [P, G4, B])
        fi = sb("fi", [P, 2, B])
        tanhc = sb("tanhc", [P, B])
        h2 = sb("h2", [P, 2, B])
        h_hi = sb("h_hi", [P, 2, B], F16)
        h_lo = sb("h_lo", [P, 2, B], F16)
        lnbn = sb("lnbn", [P, 6])
        lnmv = sb("lnmv", [P, 2])
        lnve = sb("lnve", [P, 1])
        lnrs = sb("lnrs", [P, 1])
        xf = sb("xf", [P, D])
        xf_hi = sb("xf_hi", [P, 2, P], F16)
        xf_lo = sb("xf_lo", [P, 2, P], F16)
        zT = sb("zT", [GH + 1, P])
        top = sb("top", [P, NE])
        top_i = sb("top_i", [P, NE], U32)
        top_f = sb("top_f", [P, 2])
        nmax = sb("nmax", [P, 1])
        th = sb("th", [P, NE])
        den = sb("den", [P, NE])
        rden = sb("rden", [P, NE])
        ex = sb("ex", [P, NE])
        esum = sb("esum", [P, 1])
        rsum = sb("rsum", [P, 1])
        ngap = sb("ngap", [P, 1])
        tgap = sb("tgap", [P, 1])
        tw1 = sb("tw1", [P, 1])
        tw2 = sb("tw2", [P, 1])
        cp1 = sb("cp1", [P, NE])
        cp2 = sb("cp2", [P, NE])
        comb = sb("comb", [P, 2, NE])
        combT = sb("combT", [NE, P])
        hidT = [sb(f"hidT{k}", [P, HC, P]) for k in range(4)]

        hid_ps = [bank("hid0"), bank("hid1")]
        y_ps = [bank("y0"), bank("y1")]
        gate_ps = bank("gate_ps")
        turn_ps = bank("turn_ps")
        lg_ps = bank("lg_ps")
        cb_ps = bank("cb_ps")
        proj_ps = [cb_ps[:, 0:D], cb_ps[:, D:2 * D]] + [y_ps[k][:, 0:D] for k in (0, 1, 0)]
        pre_ps = [gate_ps, hid_ps[0], hid_ps[1], y_ps[1], cb_ps]

        load = {n: sem(f"load_{n}") for n in LOADS}
        F = {n: sem(f"f_{n}") for n in FRONT}
        S = {n: sem(n) for n in PER_TILE}
        stored = sem("stored")

        ident = cols_sb[:, C_ID:C_ID + P]
        iota = cols_sb[:, C_IOTA:C_IOTA + NE]
        gamma, beta = affine_sb[:, 0], affine_sb[:, 1]
        unscale_hh = scale_hh[:, 2:3].bitcast(F32)
        down_w1 = scale_w1[:, 0:1].bitcast(F32)
        up_w1 = scale_w1[:, 1:2].bitcast(F32)
        wih_sb = cols_sb[:, C_WIH:]
        whh_sb = xrest_sb[:, X_WHH:]
        rec_ps = gate_ps[:, 0:G4 * B].rearrange("q (g b) -> q g b", g=G4)

        def by_gate(ps, g):
            return ps[:].rearrange("q (s g b) -> q g s b", s=2, g=G4)[:, g]

        block = ctx.enter_context(nc.Block())

        @block.sync
        def _(sp):
            sp.dma_start(first_sb[:], first).then_inc(load["first"], 16)
            sp.dma_start(rows_sb[:], rows).then_inc(load["rows"], 16)
            sp.dma_start(affine_sb[:].rearrange("q a d -> q (a d)"), affine.broadcast_to([P, 2 * D])
                         ).then_inc(load["affine"], 16)
            sp.dma_start(cols_sb[:], cols).then_inc(load["cols"], 16)
            sp.dma_start(xrest_sb[:], xrest).then_inc(load["xrest"], 16)
            sp.dma_start(we1_sb[:, 0:HALF1], we1[:, 0:HALF1]).then_inc(load["we1a"], 16)
            sp.dma_start(we1_sb[:, HALF1:], we1[:, HALF1:]).then_inc(load["we1b"], 16)
            h = NE // 2
            sp.dma_start(we2_sb[:, 0:h], we2[:, 0:h]).then_inc(load["we2a"], 16)
            sp.dma_start(we2_sb[:, h:NE], we2[:, h:NE]).then_inc(load["we2b"], 16)
            for t in range(TILES):
                sp.wait_ge(S[f"acc_{NE - 1}"], t + 1)
                for p in (0, 1):
                    sp.dma_start(out[:, 2 * t + p, :], res[p * B:(p + 1) * B, t, :]).then_inc(stored, 16)
            sp.wait_ge(stored, 16 * PATCHES)

        @block.gpsimd
        def _(pool):
            nc.gpsimd.memset(ones[:], 1.0).then_inc(F["ones"], 1)
            nc.gpsimd.memset(neg_half[:], -0.5).then_inc(F["neg_half"], 1)
            nc.gpsimd.memset(cell[0][:, 0, :], 0.0).then_inc(F["cell_zero"], 1)
            pool.wait_ge(F["cell_zero"], 1)
            nc.gpsimd.memset(zT[GH:GH + 1, :], 1.0).then_inc(F["z_one"], 1)
            pool.wait_ge(F["z_one"], 1)
            pool.wait_ge(F["neg_half"], 1)

            def rstd_of(t, ln):
                pool.wait_ge(S[f"ve_{ln}"], t + 1)
                nc.gpsimd.tensor_tensor(rstd[:, t:t + 1], ve[:, t:t + 1], neg_half[:], ALU.pow
                                        ).then_inc(S[f"rstd_{ln}"], 1)

            def ln_rstd(t):
                pool.wait_ge(S["ln_var"], t + 1)
                nc.gpsimd.tensor_tensor(lnrs[:], lnve[:], neg_half[:, 0:1], ALU.pow).then_inc(S["ln_rstd"], 1)

            def add_bias(t):
                pool.wait_ge(S["xg"], t + 1)
                nc.gpsimd.tensor_tensor(xg[:, t], xg[:, t], bias[:].unsqueeze(1).unsqueeze(3).to_broadcast([P, 2, G4, B]),
                                        ALU.add).then_inc(S["biased"], 1)

            def hidden_low(t, p):
                pool.wait_ge(S[f"h_hi{p}"], t + 1)
                pool.wait_ge(S[f"h_ready{p}"], t + 1)
                if t >= 1:
                    pool.wait_ge(S[f"rec_done{1 - p}"], t)
                nc.gpsimd.tensor_tensor(h_lo[:, p, :], h2[:, p, :], h_hi[:, p, :], ALU.subtract
                                        ).then_inc(S[f"h_lo{p}"], 1)

            rstd_of(0, "a")
            rstd_of(0, "b")
            pool.wait_ge(load["cols"], 16)
            nc.gpsimd.tensor_tensor(bias[:], cols_sb[:, C_BIH:C_BIH + G4], cols_sb[:, C_BHH:C_BHH + G4], ALU.add
                                    ).then_inc(F["bias_sum"], 1)
            pool.wait_ge(F["bias_sum"], 1)
            nc.gpsimd.tensor_scalar(bias[:, 1:], bias[:, 1:], 0.5, None, ALU.mult).then_inc(F["bias_half"], 1)
            pool.wait_ge(F["bias_half"], 1)
            rstd_of(1, "a")
            rstd_of(1, "b")
            rstd_of(2, "a")
            hidden_low(0, 0)
            rstd_of(2, "b")
            rstd_of(3, "a")
            hidden_low(0, 1)
            ln_rstd(0)
            hidden_low(1, 0)
            rstd_of(3, "b")
            rstd_of(4, "a")
            add_bias(2)
            hidden_low(1, 1)
            rstd_of(4, "b")
            for t in range(TILES - 1):
                ln_rstd(t + 1)
                if t + 2 < TILES:
                    hidden_low(t + 2, 0)
                    hidden_low(t + 2, 1)
                if t < 2:
                    add_bias(3 + t)

        @block.tensor
        def _(pe):
            def chunks(t, k):
                c = (2 * t + k) * B
                return first_sb[:, c:c + 2 * B] if c < 2 * B else xrest_sb[:, c - 3 * B:c - B]

            def project(t):
                pe.matmul(proj_ps[t], ones[0:1, :], rows_sb[0:1, R_TOKB:R_TOKB + D], start=True, stop=False)
                if t == 1:
                    for b in (0, 1):
                        lhs = first_sb[:, 2 * B:3 * B] if b == 0 else xrest_sb[:, 0:B]
                        pe.matmul(proj_ps[t][b * B:(b + 1) * B], lhs, first_sb[:, A_W:A_W + D],
                                  start=False, stop=False)
                else:
                    pe.matmul(proj_ps[t], chunks(t, 0), first_sb[:, A_W:A_W + D], start=False, stop=False)
                pe.matmul(proj_ps[t], chunks(t, 1), first_sb[:, A_W + D:A_W + 2 * D], start=False, stop=True
                          ).then_inc(S["proj"], 1)

            def warm(n):
                for _ in range(n):
                    pe.matmul(lg_ps[:, 384:512], idle[:], idle[:], start=True, stop=True)

            def gate_bias(t):
                for g in range(G4):
                    pe.matmul(by_gate(pre_ps[t], g), rows_sb[0:2, R_LSTMB + g * D:R_LSTMB + (g + 1) * D],
                              ones[0:2, :], start=g == 0, stop=False, skip_group_check=True)

            def turn_xn(t):
                pe.wait_ge(S["xn"], t + 1)
                if t >= 1:
                    pe.wait_ge(S["xnT"], t)
                pe.transpose(turn_ps[:, 0:P], xn[:, t, :], ident).then_inc(S["turned"], 1)

            def gate_inputs(t):
                pe.wait_ge(S["xnT"], t + 1)
                for g in range(G4):
                    mm = pe.matmul(by_gate(pre_ps[t], g), wih_sb[:, g * D:(g + 1) * D], xnT[:, t, :],
                                   start=t >= 2 and g == 0, stop=True, skip_group_check=True)
                mm.then_inc(S["pre"], 1)

            def recur(t, p):
                q, n = 1 - p, t + p
                pe.wait_ge(S[f"h_hi{q}"], n)
                for g in range(G4):
                    for w in (whh_hi, whh_lo):
                        pe.matmul(rec_ps[:, g, :], w[:, g * D:(g + 1) * D], h_hi[:, q, :],
                                  start=g == 0 and w is whh_hi, stop=False, skip_group_check=True)
                pe.wait_ge(S[f"h_lo{q}"], n)
                for g in range(G4):
                    mm = pe.matmul(rec_ps[:, g, :], whh_hi[:, g * D:(g + 1) * D], h_lo[:, q, :],
                                   start=False, stop=True, skip_group_check=True)
                mm.then_inc(S[f"rec_done{p}"], 1)

            def turn_h(t):
                pe.wait_ge(S["h_ready1"], t + 1)
                if t >= 1:
                    pe.wait_ge(S["xf_lo"], t)
                pe.transpose(turn_ps[:, 0:P], h2[:].rearrange("q s b -> q (s b)"), ident).then_inc(S["hs_turned"], 1)

            def turn_xf(t):
                pe.wait_ge(S["xf_ready"], t + 1)
                pe.transpose(turn_ps[:, P:2 * P], xf[:], ident).then_inc(S["xf_turned"], 1)

            def three(dst, c0, c1, t):
                pe.matmul(dst, we1_hi[:, c0:c1], xf_hi[:, t % 2], start=True, stop=False)
                pe.matmul(dst, we1_hi[:, c0:c1], xf_lo[:, t % 2], start=False, stop=False)
                return pe.matmul(dst, we1_lo[:, c0:c1], xf_hi[:, t % 2], start=False, stop=True)

            def split_part(k):
                pe.wait_ge(F["w1_hi"], k + 1)
                pe.wait_ge(F["w1_lo"], k + 1)

            def gate_hidden(t):
                pe.wait_ge(S["xf_hi"], t + 1)
                pe.wait_ge(S["xf_lo"], t + 1)
                if t == 0:
                    split_part(0)
                if t >= 1:
                    pe.wait_ge(S["top_index"], t)
                three(lg_ps[0:GH, 0:P], 0, GH, t).then_inc(S["z_done"], 1)

            def gate_logits(t):
                pe.wait_ge(S["z_ready"], t + 1)
                pe.matmul(lg_ps[:, P:P + NE], zT[:], cols_sb[0:GH + 1, C_GW2:C_GW2 + NE], start=True, stop=True
                          ).then_inc(S["logits_done"], 1)

            def turn_comb(t):
                pe.wait_ge(S["comb"], t + 1)
                if t >= 1:
                    pe.wait_ge(S["bias_added"], t)
                pe.transpose(cb_ps[0:NE, 0:P], comb[:, t % 2], ident).then_inc(S["comb_turned"], 1)

            def expert_bias(t):
                pe.wait_ge(S["combT_ready"], t + 1)
                pe.matmul(cb_ps[:, P:2 * P], combT[:], rows_sb[:, R_BE2:R_BE2 + D], start=True, stop=True
                          ).then_inc(S["bias_done"], 1)

            def mm1(t, e):
                if e >= 2:
                    pe.wait_ge(S[f"gelu_{e - 2}"], t + 1)
                elif t >= 1:
                    pe.wait_ge(S[f"gelu_{NE - 2 + e}"], t)
                if t == 0 and e % 2 == 0:
                    split_part(e // 2)
                for j in range(HC):
                    c = GH + (HC * e + j) * P
                    mm = three(hid_ps[e % 2][:, j * P:(j + 1) * P], c, c + P, t)
                mm.then_inc(S[f"mm1_{e}"], 1)

            def mm2(t, e):
                pe.wait_ge(S[f"gelu_{e}"], t + 1)
                if e % 2 == 0 and e >= 4:
                    pe.wait_ge(S[f"acc_{e - 3}"], t + 1)
                elif e % 2 == 0 and t >= 1:
                    pe.wait_ge(S[f"acc_{NE - 3 + e}"], t)
                elif e == 2:
                    pe.wait_ge(S["xg"], 4)
                for j in range(HC):
                    mm = pe.matmul(y_ps[e // 2 % 2][:, (e % 2) * D:(e % 2 + 1) * D], hidT[e % 4][:, j, :],
                                   we2_sb[:, e, j, :], start=j == 0, stop=j == 1)
                mm.then_inc(S[f"mm2_{e}"], 1)

            pe.wait_ge(F["idle"], 1)
            warm(WARM[0])
            pe.wait_ge(F["ones"], 1)
            pe.wait_ge(load["first"], 16)
            pe.wait_ge(load["rows"], 16)
            project(0)
            warm(WARM[1])
            pe.wait_ge(F["bias_scaled"], 1)
            gate_bias(0)
            pe.wait_ge(load["xrest"], 16)
            pe.wait_ge(S["centred"], 1)
            project(1)
            pe.wait_ge(F["sq_hh"], 1)
            pe.matmul(turn_ps[:, 511:512], ones[:], sumsq_hh[:], start=True, stop=True).then_inc(F["norm_hh"], 1)
            project(2)
            warm(WARM[2])
            pe.wait_ge(load["cols"], 16)
            pe.wait_ge(F["wih_scaled"], 1)
            pe.wait_ge(F["hh_v"], 1)
            turn_xn(0)
            gate_inputs(0)
            gate_bias(1)
            project(3)
            turn_xn(1)
            gate_inputs(1)
            warm(WARM[3])
            pe.wait_ge(S["xg"], 1)
            pe.wait_ge(F["hh_hi"], 1)
            pe.wait_ge(F["hh_lo"], 1)
            recur(0, 1)
            pe.wait_ge(S["centred"], 3)
            project(4)
            turn_xn(2)
            gate_inputs(2)
            warm(WARM[4])
            pe.wait_ge(S["xnT"], 3)
            recur(1, 0)
            turn_h(0)
            warm(WARM[5])
            turn_xf(0)
            recur(1, 1)
            gate_hidden(0)
            turn_xn(3)
            gate_inputs(3)
            gate_logits(0)
            turn_xn(4)
            gate_inputs(4)
            warm(WARM[6])
            for n in ("we2a", "we2b"):
                pe.wait_ge(load[n], 16)
            pe.wait_ge(S["xg"], 3)

            def iteration(t):
                before, now, after, lstm = t >= 1, t < TILES, t + 1 < TILES, t + 2 < TILES
                if now:
                    mm1(t, 0)
                if after:
                    turn_h(t + 1)
                if now:
                    mm1(t, 1)
                if lstm:
                    recur(t + 2, 0)
                if before:
                    mm2(t - 1, 6)
                    mm2(t - 1, 7)
                if now:
                    mm1(t, 2)
                    mm1(t, 3)
                    mm2(t, 0)
                    mm2(t, 1)
                if after:
                    turn_xf(t + 1)
                if now:
                    mm1(t, 4)
                    mm1(t, 5)
                    mm2(t, 2)
                if after:
                    gate_hidden(t + 1)
                if lstm:
                    recur(t + 2, 1)
                if now:
                    mm2(t, 3)
                if after:
                    gate_logits(t + 1)
                if t == 0:
                    pe.wait_ge(S["xg"], TILES)
                if now:
                    turn_comb(t)
                    mm1(t, 6)
                    mm1(t, 7)
                    expert_bias(t)
                    mm2(t, 4)
                    mm2(t, 5)

            for t in range(TILES + 1):
                iteration(t)

        @block.scalar
        def _(act):
            act.wait_ge(F["neg_half"], 1)
            nc.scalar.activation(tgap[:], neg_half[:], ACT.Gelu).then_inc(F["table"], 1)

            def xnT_copy(t):
                act.wait_ge(S["turned"], t + 1)
                nc.scalar.copy(xnT[:, t, :], turn_ps[:, 0:P]).then_inc(S["xnT"], 1)

            def xg_copy(t):
                act.wait_ge(S["pre"], t + 1)
                nc.scalar.copy(xg[:, t].rearrange("q s g b -> q (s g b)"), pre_ps[t][:]).then_inc(S["xg"], 1)

            def gates(t, p, src, ready, n):
                act.wait_ge(ready, n)
                if t >= 1 or p == 1:
                    act.wait_ge(S[f"h_ready{1 - p}"], t + p)
                nc.scalar.activation(cell[p][:, 1:5, :], src, ACT.Tanh).then_inc(S[f"gates_ready{p}"], 1)

            def tanh_cell(t, p):
                act.wait_ge(S[f"cell_ready{p}"], t + 1)
                if t >= 1 or p == 1:
                    act.wait_ge(S[f"h_ready{1 - p}"], t + p)
                nc.scalar.activation(tanhc[:], cell[1 - p][:, 0, :], ACT.Tanh, scale=0.5
                                     ).then_inc(S[f"tanhc_ready{p}"], 1)

            act.wait_ge(load["rows"], 16)
            nc.scalar.mul(rows_sb[0:2, R_LSTMB + D:], rows_sb[0:2, R_LSTMB + D:], 0.5).then_inc(F["bias_scaled"], 1)
            act.wait_ge(load["cols"], 16)
            nc.scalar.mul(wih_sb[:, D:], wih_sb[:, D:], 0.5).then_inc(F["wih_scaled"], 1)
            act.wait_ge(load["xrest"], 16)
            nc.scalar.activation(squares[:, 0:G4 * D], whh_sb, ACT.Square, accum_out=sumsq_hh[:]
                                 ).then_inc(F["sq_hh"], 1)
            act.wait_ge(F["hh_scale"], 1)
            nc.scalar.activation(whh_hi[:, 0:D], whh_sb[:, 0:D], ACT.Copy, scale=scale_hh[:, 0:1].bitcast(F32))
            nc.scalar.activation(whh_hi[:, D:], whh_sb[:, D:], ACT.Copy, scale=scale_hh[:, 1:2].bitcast(F32)
                                 ).then_inc(F["hh_hi"], 1)
            xnT_copy(0)

            def square_w1(k, c0, c1):
                act.wait_ge(load[f"we1{'ab'[k]}"], 16)
                act.wait_ge(F["sq_hh"] if k == 0 else F["sq_w1"], 1)
                nc.scalar.activation(squares[:, 0:c1 - c0], we1_sb[:, c0:c1], ACT.Square,
                                     accum_out=sumsq_w1[:, k:k + 1]).then_inc(F["sq_w1"], 1)

            def w1_high(k):
                c0, c1 = PART_ENDS[k:k + 2]
                if k == 0:
                    act.wait_ge(F["w1_scale"], 1)
                nc.scalar.activation(we1_hi[:, c0:c1], we1_sb[:, c0:c1], ACT.Copy, scale=down_w1
                                     ).then_inc(F["w1_hi"], 1)

            square_w1(0, 0, HALF1)
            gates(0, 0, rec_ps, S["pre"], 1)
            xg_copy(0)
            tanh_cell(0, 0)
            xnT_copy(1)
            square_w1(1, HALF1, W1)
            gates(0, 1, pre[:], S["pre_ready1"], 1)
            xg_copy(1)
            tanh_cell(0, 1)
            xnT_copy(2)
            w1_high(0)
            xg_copy(2)
            w1_high(1)

            def xf_high(t):
                act.wait_ge(S["xf_turned"], t + 1)
                if t >= 2:
                    act.wait_ge(S[f"mm1_{NE - 1}"], t - 1)
                nc.scalar.activation(xf_hi[:, t % 2], turn_ps[:, P:2 * P], ACT.Copy, scale=up_w1).then_inc(S["xf_hi"], 1)

            def gelu(t, e):
                act.wait_ge(S[f"mm1_{e}"], t + 1)
                if e >= 4:
                    act.wait_ge(S[f"mm2_{e - 4}"], t + 1)
                elif t >= 1:
                    act.wait_ge(S[f"mm2_{e + 4}"], t)
                for j in range(HC):
                    c = C_BE1 + HC * e + j
                    a = nc.scalar.activation(hidT[e % 4][:, j, :], hid_ps[e % 2][:, j * P:(j + 1) * P], ACT.Gelu,
                                             bias=cols_sb[:, c:c + 1], scale=W1_BACK)
                a.then_inc(S[f"gelu_{e}"], 1)

            def z(t):
                act.wait_ge(S["z_done"], t + 1)
                if t >= 1:
                    act.wait_ge(S["logits_done"], t)
                nc.scalar.activation(zT[0:GH, :], lg_ps[0:GH, 0:P], ACT.Relu, bias=cols_sb[0:GH, C_GB1:C_GB1 + 1],
                                     scale=W1_BACK).then_inc(S["z_ready"], 1)

            def tanh_logits(t):
                act.wait_ge(S["neg_max"], t + 1)
                nc.scalar.activation(th[:], top[:], ACT.Tanh, bias=nmax[:], scale=0.5).then_inc(S["tanh_logits"], 1)

            def tanh_gap(t):
                act.wait_ge(S["gap"], t + 1)
                nc.scalar.activation(tgap[:], ngap[:], ACT.Tanh, scale=-0.5).then_inc(S["gap_tanh"], 1)

            def combT_copy(t):
                act.wait_ge(S["comb_turned"], t + 1)
                if t >= 1:
                    act.wait_ge(S["bias_done"], t)
                nc.scalar.copy(combT[:], cb_ps[0:NE, 0:P]).then_inc(S["combT_ready"], 1)

            gates(1, 0, pre[:], S["pre_ready0"], 1)
            w1_high(2)
            tanh_cell(1, 0)
            w1_high(3)
            xf_high(0)
            gates(1, 1, pre[:], S["pre_ready1"], 2)
            z(0)
            xnT_copy(3)
            tanh_cell(1, 1)
            xg_copy(3)
            xnT_copy(4)
            xg_copy(4)
            tanh_logits(0)

            def iteration(t):
                after, lstm = t + 1 < TILES, t + 2 < TILES
                gelu(t, 0)
                tanh_gap(t)
                gelu(t, 1)
                if lstm:
                    gates(t + 2, 0, pre[:], S["pre_ready0"], t + 2)
                gelu(t, 2)
                gelu(t, 3)
                if lstm:
                    tanh_cell(t + 2, 0)
                if after:
                    xf_high(t + 1)
                gelu(t, 4)
                if after:
                    z(t + 1)
                gelu(t, 5)
                combT_copy(t)
                if lstm:
                    gates(t + 2, 1, pre[:], S["pre_ready1"], t + 3)
                if after:
                    tanh_logits(t + 1)
                gelu(t, 6)
                if lstm:
                    tanh_cell(t + 2, 1)
                gelu(t, 7)

            for t in range(TILES):
                iteration(t)

        @block.vector
        def _(dve):
            def once(ins, name):
                ins.then_inc(F[name], 1)
                dve.wait_ge(F[name], 1)

            def step(ins, name, t):
                ins.then_inc(S[name], 1)
                dve.wait_ge(S[name], t + 1)

            def centre_scale(dst, src, mean, rs):
                return nc.vector.tensor_scalar(dst, src, mean, rs, ALU.subtract, ALU.mult)

            def forget_input(t, p):
                dve.wait_ge(S[f"gates_ready{p}"], t + 1)
                nc.vector.scalar_tensor_tensor(fi[:], cell[p][:, 2:4, :], 1.0, cell[p][:, 0:2, :],
                                               ALU.add, ALU.mult).then_inc(S[f"fi_ready{p}"], 1)

            def new_cell(t, p):
                dve.wait_ge(S[f"fi_ready{p}"], t + 1)
                nc.vector.scalar_tensor_tensor(cell[1 - p][:, 0, :], fi[:, 0, :], 0.5, fi[:, 1, :],
                                               ALU.mult, ALU.add).then_inc(S[f"cell_ready{p}"], 1)

            def hidden(t, p):
                dve.wait_ge(S[f"tanhc_ready{p}"], t + 1)
                if t >= 1:
                    dve.wait_ge(S[f"rec_done{1 - p}"], t)
                    dve.wait_ge(S[f"h_lo{p}"], t)
                    dve.wait_ge(S["hs_turned"], t)
                o = cell[p][:, 4, :]
                nc.vector.scalar_tensor_tensor(h_hi[:, p, :], o, 1.0, tanhc[:], ALU.add, ALU.mult
                                               ).then_inc(S[f"h_hi{p}"], 1)
                nc.vector.scalar_tensor_tensor(h2[:, p, :], o, 1.0, tanhc[:], ALU.add, ALU.mult
                                               ).then_inc(S[f"h_ready{p}"], 1)

            def add_pre(t, p):
                if t >= 2 and p == 0:
                    dve.wait_ge(S["biased"], t - 1)
                elif t < 2:
                    dve.wait_ge(S["xg"], t + 1)
                n = t if p == 0 else t + 1
                dve.wait_ge(S[f"rec_done{p}"], n)
                if t >= 1:
                    dve.wait_ge(S[f"gates_ready{1 - p}"], t + p)
                nc.vector.scalar_tensor_tensor(pre[:], rec_ps, unscale_hh, xg[:, t, p], ALU.mult, ALU.add
                                               ).then_inc(S[f"pre_ready{p}"], 1)

            def front(t, stage):
                def named(ins, name):
                    ins.then_inc(S[name], 1)

                def after(name):
                    dve.wait_ge(S[name], t + 1)

                ps, row = proj_ps[t], res[:, t, :]
                mean, var, rs = mv[:, t, 0:1], mv[:, t, 1:2], rstd[:, t:t + 1]
                if stage == 0:
                    after("proj")
                    named(nc.vector.bn_stats(bn[:, t, :], ps), "stats_a")
                elif stage == 1:
                    after("stats_a")
                    named(nc.vector.bn_aggr(mv[:, t, :], bn[:, t, :]), "mean_a")
                elif stage == 2:
                    after("mean_a")
                    named(nc.vector.tensor_scalar(ve[:, t:t + 1], var, TOK_EPS, None, ALU.add), "ve_a")
                    dve.wait_ge(load["affine"], 16)
                    named(nc.vector.scalar_tensor_tensor(centred[:, t, :], ps, mean, gamma, ALU.subtract, ALU.mult),
                          "centred")
                elif stage == 3:
                    after("rstd_a")
                    after("centred")
                    named(nc.vector.scalar_tensor_tensor(row, centred[:, t, :], rs, beta, ALU.mult, ALU.add), "res")
                elif stage == 4:
                    after("res")
                    named(nc.vector.bn_stats(bn[:, t, :], row), "stats_b")
                elif stage == 5:
                    after("stats_b")
                    named(nc.vector.bn_aggr(mv[:, t, :], bn[:, t, :]), "mean_b")
                elif stage == 6:
                    after("mean_b")
                    named(nc.vector.tensor_scalar(ve[:, t:t + 1], var, LN_EPS, None, ALU.add), "ve_b")
                else:
                    after("rstd_b")
                    named(centre_scale(xn[:, t, :], row, mean, rs), "xn")

            def fronts(*stages):
                for t, stage in stages:
                    front(t, stage)

            nc.vector.memset(idle[:], 1.0).then_inc(F["idle"], 1)
            fronts((0, 0), (0, 1), (0, 2), (0, 3), (0, 4), (0, 5), (0, 6))
            dve.wait_ge(F["norm_hh"], 1)
            once(nc.vector.tensor_scalar(v_hh[:], turn_ps[:, 511:512].bitcast(U32), 24, None,
                                         ALU.logical_shift_right), "hh_v")
            for k, (sign, bits) in enumerate(((-1, HH_TO - EXP1), (-1, HH_TO - 2 * EXP1), (1, HH_BACK))):
                last = nc.vector.tensor_scalar(scale_hh[:, k:k + 1], v_hh[:], sign * EXP1, bits, ALU.mult, ALU.add)
            once(last, "hh_scale")
            fronts((0, 7), (1, 0), (1, 1), (1, 2), (2, 0), (1, 3), (1, 4), (2, 1), (1, 5), (2, 2), (1, 6))
            dve.wait_ge(F["hh_hi"], 1)
            for c0, c1, k in ((0, D, 0), (D, G4 * D, 1)):
                last = nc.vector.scalar_tensor_tensor(whh_lo[:, c0:c1], whh_sb[:, c0:c1],
                                                      scale_hh[:, k:k + 1].bitcast(F32), whh_hi[:, c0:c1],
                                                      ALU.mult, ALU.subtract)
            last.then_inc(F["hh_lo"], 1)
            fronts((1, 7))
            dve.wait_ge(F["cell_zero"], 1)
            forget_input(0, 0)
            new_cell(0, 0)
            fronts((2, 3))
            hidden(0, 0)
            fronts((2, 4), (2, 5), (2, 6))
            add_pre(0, 1)
            fronts((3, 0), (2, 7))
            dve.wait_ge(F["sq_w1"], 2)
            once(nc.vector.tensor_tensor(sumsq_w1[:, 2:3], sumsq_w1[:, 0:1], sumsq_w1[:, 1:2], ALU.add), "w1_sum")
            once(nc.vector.tensor_scalar(v_w1[:, 0:1], sumsq_w1[:, 2:3].bitcast(U32), 24, None,
                                         ALU.logical_shift_right), "w1_v")
            once(nc.vector.tensor_scalar(v_w1[:, 1:2], v_w1[:, 0:1], -W1_FROM, 0.0, ALU.add, ALU.max), "w1_k")
            once(nc.vector.tensor_scalar(v_w1[:, 2:3], v_w1[:, 1:2], W1_MOST, EXP1, ALU.min, ALU.mult), "w1_exp")
            for k, (sign, bits) in enumerate(((-1.0, (127 + W1_UP) * EXP1), (1.0, 127 * EXP1))):
                last = nc.vector.tensor_scalar(scale_w1[:, k:k + 1], v_w1[:, 2:3], sign, bits, ALU.mult, ALU.add)
            once(last, "w1_scale")
            forget_input(0, 1)
            new_cell(0, 1)
            fronts((3, 1), (3, 2))
            hidden(0, 1)

            def w1_low(k):
                c0, c1 = PART_ENDS[k:k + 2]
                dve.wait_ge(F["w1_hi"], k + 1)
                nc.vector.scalar_tensor_tensor(we1_lo[:, c0:c1], we1_sb[:, c0:c1], down_w1, we1_hi[:, c0:c1],
                                               ALU.mult, ALU.subtract).then_inc(F["w1_lo"], 1)

            def add_h(t):
                dve.wait_ge(S["hs_turned"], t + 1)
                nc.vector.scalar_tensor_tensor(res[:, t, :], turn_ps[:, 0:P], 0.5, res[:, t, :], ALU.mult, ALU.add
                                               ).then_inc(S["h_added"], 1)

            def ln_moments(t):
                dve.wait_ge(S["h_added"], t + 1)
                nc.vector.bn_stats(lnbn[:], res[:, t, :]).then_inc(S["ln_stats"], 1)

            def ln_mean(t):
                dve.wait_ge(S["ln_stats"], t + 1)
                nc.vector.bn_aggr(lnmv[:], lnbn[:]).then_inc(S["ln_mean"], 1)

            def ln_var(t):
                dve.wait_ge(S["ln_mean"], t + 1)
                nc.vector.tensor_scalar(lnve[:], lnmv[:, 1:2], LN_EPS, None, ALU.add).then_inc(S["ln_var"], 1)

            def ln_out(t):
                dve.wait_ge(S["ln_rstd"], t + 1)
                if t >= 1:
                    dve.wait_ge(S["xf_turned"], t)
                centre_scale(xf[:], res[:, t, :], lnmv[:, 0:1], lnrs[:]).then_inc(S["xf_ready"], 1)

            def xf_low(t):
                dve.wait_ge(S["xf_hi"], t + 1)
                if t >= 2:
                    dve.wait_ge(S[f"mm1_{NE - 1}"], t - 1)
                nc.vector.scalar_tensor_tensor(xf_lo[:, t % 2], turn_ps[:, P:2 * P], up_w1, xf_hi[:, t % 2],
                                               ALU.mult, ALU.subtract).then_inc(S["xf_lo"], 1)

            def top_sort(t):
                dve.wait_ge(S["logits_done"], t + 1)
                nc.vector.max(top[:], lg_ps[:, P:P + NE]).then_inc(S["top_found"], 1)

            def top_where(t):
                dve.wait_ge(S["top_found"], t + 1)
                nc.vector.tensor_scalar(nmax[:], top[:, 0:1], -0.5, None, ALU.mult).then_inc(S["neg_max"], 1)
                nc.vector.max_index(top_i[:], top[:], lg_ps[:, P:P + NE]).then_inc(S["top_index"], 1)

            def softmax_1(t):
                dve.wait_ge(S["tanh_logits"], t + 1)
                nc.vector.tensor_scalar(den[:], th[:], -1.0, 1.0, ALU.mult, ALU.add).then_inc(S["one_minus"], 1)

            def softmax_2(t):
                dve.wait_ge(S["one_minus"], t + 1)
                nc.vector.reciprocal(rden[:], den[:]).then_inc(S["one_minus_inv"], 1)

            def softmax_3(t):
                dve.wait_ge(S["one_minus_inv"], t + 1)
                nc.vector.scalar_tensor_tensor(ex[:], th[:], 1.0, rden[:], ALU.add, ALU.mult).then_inc(S["exps"], 1)

            def softmax_4(t):
                dve.wait_ge(S["exps"], t + 1)
                nc.vector.tensor_reduce(esum[:], ex[:], AX.X, ALU.add).then_inc(S["exp_sum"], 1)

            def softmax_5(t):
                dve.wait_ge(S["exp_sum"], t + 1)
                nc.vector.reciprocal(rsum[:], esum[:]).then_inc(S["exp_sum_inv"], 1)

            def softmax_6(t):
                dve.wait_ge(S["exp_sum_inv"], t + 1)
                nc.vector.scalar_tensor_tensor(ngap[:], ex[:, 1:2], -1.0, rsum[:], ALU.add, ALU.mult
                                               ).then_inc(S["gap"], 1)
                dve.wait_ge(S["top_index"], t + 1)
                nc.vector.tensor_copy(top_f[:], top_i[:, 0:2]).then_inc(S["index_f"], 1)

            def combine_1(t):
                dve.wait_ge(S["gap_tanh"], t + 1)
                nc.vector.tensor_scalar(tw1[:], tgap[:], 0.5, 0.5, ALU.mult, ALU.add).then_inc(S["weight1"], 1)
                nc.vector.tensor_scalar(tw2[:], tgap[:], -0.5, 0.5, ALU.mult, ALU.add).then_inc(S["weight2"], 1)

            def combine_2(t):
                dve.wait_ge(S["index_f"], t + 1)
                dve.wait_ge(S["weight1"], t + 1)
                nc.vector.tensor_scalar(cp1[:], iota, top_f[:, 0:1], tw1[:], ALU.is_equal, ALU.mult
                                        ).then_inc(S["part1"], 1)
                dve.wait_ge(S["weight2"], t + 1)
                nc.vector.tensor_scalar(cp2[:], iota, top_f[:, 1:2], tw2[:], ALU.is_equal, ALU.mult
                                        ).then_inc(S["part2"], 1)

            def combine_3(t):
                dve.wait_ge(S["part1"], t + 1)
                dve.wait_ge(S["part2"], t + 1)
                if t >= 2:
                    dve.wait_ge(S[f"acc_{NE - 1}"], t - 1)
                    dve.wait_ge(S["comb_turned"], t - 1)
                nc.vector.tensor_tensor(comb[:, t % 2], cp1[:], cp2[:], ALU.add).then_inc(S["comb"], 1)

            def add_bias(t):
                dve.wait_ge(S["bias_done"], t + 1)
                dve.wait_ge(S["acc_3"], t + 1)
                nc.vector.tensor_tensor(res[:, t, :], res[:, t, :], cb_ps[:, P:2 * P], ALU.add
                                        ).then_inc(S["bias_added"], 1)

            def accumulate(t, e):
                dve.wait_ge(S[f"mm2_{e | 1}"], t + 1)
                if e == 4:
                    dve.wait_ge(S["bias_added"], t + 1)
                elif e >= 1:
                    dve.wait_ge(S[f"acc_{e - 1}"], t + 1)
                else:
                    dve.wait_ge(S["comb"], t + 1)
                nc.vector.scalar_tensor_tensor(res[:, t, :], y_ps[e // 2 % 2][:, (e % 2) * D:(e % 2 + 1) * D],
                                               comb[:, t % 2, e:e + 1], res[:, t, :], ALU.mult, ALU.add
                                               ).then_inc(S[f"acc_{e}"], 1)

            add_pre(1, 0)
            add_h(0)
            fronts((3, 3))
            ln_moments(0)
            fronts((3, 4))
            ln_mean(0)
            forget_input(1, 0)
            ln_var(0)
            new_cell(1, 0)
            w1_low(0)
            ln_out(0)
            hidden(1, 0)
            fronts((3, 5), (4, 0), (3, 6), (4, 1))
            w1_low(1)
            fronts((4, 2))
            xf_low(0)
            add_pre(1, 1)
            fronts((3, 7), (4, 3))
            w1_low(2)
            forget_input(1, 1)
            fronts((4, 4))
            new_cell(1, 1)
            fronts((4, 5), (4, 6))
            hidden(1, 1)
            top_sort(0)
            w1_low(3)
            top_where(0)
            fronts((4, 7))
            for softmax in (softmax_1, softmax_2, softmax_3, softmax_4, softmax_5):
                softmax(0)

            def iteration(t):
                before, now, after, lstm = t >= 1, t < TILES, t + 1 < TILES, t + 2 < TILES
                if after:
                    add_h(t + 1)
                if now:
                    softmax_6(t)
                if after:
                    ln_moments(t + 1)
                    ln_mean(t + 1)
                if before:
                    accumulate(t - 1, 5)
                if now:
                    combine_1(t)
                if lstm:
                    add_pre(t + 2, 0)
                if after:
                    ln_var(t + 1)
                if now:
                    combine_2(t)
                if before:
                    accumulate(t - 1, 6)
                if lstm:
                    forget_input(t + 2, 0)
                if after:
                    ln_out(t + 1)
                if now:
                    combine_3(t)
                if lstm:
                    new_cell(t + 2, 0)
                if before:
                    accumulate(t - 1, 7)
                if lstm:
                    hidden(t + 2, 0)
                if after:
                    xf_low(t + 1)
                if now:
                    accumulate(t, 0)
                    accumulate(t, 1)
                if lstm:
                    add_pre(t + 2, 1)
                if after:
                    top_sort(t + 1)
                if now:
                    accumulate(t, 2)
                if after:
                    top_where(t + 1)
                if now:
                    accumulate(t, 3)
                if lstm:
                    forget_input(t + 2, 1)
                if after:
                    softmax_1(t + 1)
                if lstm:
                    new_cell(t + 2, 1)
                if after:
                    softmax_2(t + 1)
                if now:
                    add_bias(t)
                if after:
                    softmax_3(t + 1)
                if lstm:
                    hidden(t + 2, 1)
                if after:
                    softmax_4(t + 1)
                if now:
                    accumulate(t, 4)
                if after:
                    softmax_5(t + 1)

            for t in range(TILES + 1):
                iteration(t)


WARM = (24, 20, 10, 10, 10, 10, 10)


def kernel(x, L0_tok_W, L0_tok_b, L0_tok_gamma, L0_tok_beta, L0_attn_W_ih, L0_attn_W_hh, L0_attn_b_ih,
           L0_attn_b_hh, L0_ffn_gw1, L0_ffn_gb1, L0_ffn_gw2, L0_ffn_gb2, L0_ffn_we1, L0_ffn_be1, L0_ffn_we2,
           L0_ffn_be2):
    import numpy as np
    import concourse.bacc as bacc
    from concourse.bass_utils import run_bass_kernel_spmd

    f = np.float32
    order = (2, 1, 0, 3)

    def by_gate(a):
        return np.concatenate([np.asarray(a).reshape(4, D, -1)[g] for g in order], axis=0)

    xs = np.asarray(x).reshape(B, -1)[:, :CHUNKS * STRIDE].reshape(B, CHUNKS, STRIDE).transpose(2, 1, 0)
    b_ih, b_hh = by_gate(L0_attn_b_ih).reshape(4, D), by_gate(L0_attn_b_hh).reshape(4, D)
    cols = np.zeros((P, C_COLS), f)
    cols[:, C_ID:C_ID + P] = np.eye(P, dtype=f)
    cols[:, C_WIH:] = by_gate(L0_attn_W_ih).T
    cols[:, C_BIH:C_BIH + G4] = b_ih.T
    cols[:, C_BHH:C_BHH + G4] = b_hh.T
    cols[:, C_BE1:C_BE1 + NE * HC] = np.asarray(L0_ffn_be1).reshape(NE * HC, P).T
    cols[:, C_IOTA:C_IOTA + NE] = np.arange(NE, dtype=f)
    cols[:GH, C_GB1] = np.asarray(L0_ffn_gb1)
    cols[:GH, C_GW2:C_GW2 + NE] = np.asarray(L0_ffn_gw2)
    cols[GH, C_GW2:C_GW2 + NE] = np.asarray(L0_ffn_gb2)
    rows = np.zeros((NE, R_COLS), f)
    rows[:, R_BE2:R_BE2 + D] = np.asarray(L0_ffn_be2)
    rows[0, R_TOKB:R_TOKB + D] = np.asarray(L0_tok_b)
    rows[0, R_LSTMB:] = b_ih.reshape(-1)
    rows[1, R_LSTMB:] = b_hh.reshape(-1)
    we1 = np.asarray(L0_ffn_we1).transpose(1, 0, 2).reshape(D, W1 - GH)
    xs = xs.reshape(P, CHUNKS * B)
    wtok = np.asarray(L0_tok_W).reshape(2, P, D).transpose(1, 0, 2).reshape(P, 2 * D)
    arrays = {
        "first": np.concatenate([xs[:, :3 * B], wtok], axis=1),
        "rows": rows,
        "affine": np.concatenate([np.asarray(L0_tok_gamma), np.asarray(L0_tok_beta)]).reshape(1, 2 * D),
        "cols": cols,
        "xrest": np.concatenate([xs[:, 3 * B:], by_gate(L0_attn_W_hh).T], axis=1),
        "we1": np.concatenate([np.asarray(L0_ffn_gw1), we1], axis=1),
        "we2": np.asarray(L0_ffn_we2).reshape(NE, HC, P, D).transpose(2, 0, 1, 3),
    }
    arrays = {n: np.ascontiguousarray(a) for n, a in arrays.items()}
    nc = bacc.Bacc("TRN2", target_bir_lowering=False, num_devices=1)
    args = [nc.dram_tensor(n, a.shape, F32, kind="ExternalInput").ap() for n, a in arrays.items()]
    out = nc.dram_tensor("out", (B, PATCHES, D), F32, kind="ExternalOutput").ap()
    audio_tower(nc, *args, out)
    got = run_bass_kernel_spmd(nc, [arrays], core_ids=[0])
    return got.results[0]["out"]
```

```python
from contextlib import ExitStack

import concourse.bass as bass
from concourse import mybir

F32 = mybir.dt.float32
F16 = mybir.dt.float16
U32 = mybir.dt.uint32
ALU = mybir.AluOpType
ACT = mybir.ActivationFunctionType
AX = mybir.AxisListType

P = 128
D = 128
B = 64
STRIDE = 128
PATCHES = 10
CHUNKS = PATCHES + 1
TILES = PATCHES * B // P
NE = 8
HC = 2
G4 = 4
TOK_EPS = 1e-3
LN_EPS = 1e-5
GH = 64
W1 = GH + NE * HC * P
PARTS = 4
PART_ENDS = [0] + [GH + (k + 1) * (W1 - GH) // PARTS for k in range(PARTS)]
HALF1 = PART_ENDS[PARTS // 2]

A_W = 3 * B
A_COLS = A_W + 2 * D
C_ID, C_BE1, C_IOTA, C_GB1, C_GW2, C_BIH, C_BHH, C_WIH = 0, 128, 144, 152, 153, 161, 165, 169
C_COLS = C_WIH + G4 * D
X_WHH = (CHUNKS - 3) * B
X_COLS = X_WHH + G4 * D
R_BE2, R_TOKB = 0, 128
R_COLS = R_TOKB + D

EXP1 = float(1 << 23)
HH_TO, HH_BACK = 203 * EXP1, 51 * EXP1
W1_UP = 6
W1_FROM, W1_MOST = 77.0 - W1_UP, 12.0
W1_BACK = 2.0 ** -W1_UP

LOADS = ["first", "rows", "affine", "cols", "xrest", "we1a", "we1b", "we2a", "we2b"]

FRONT = (
    ["ones", "neg_half", "cell_zero", "z_one", "bias_sum", "bias_half"]
    + ["norm_hh"]
    + ["table", "wih_scaled", "sq_hh", "sq_w1", "hh_hi", "w1_hi"]
    + ["idle", "hh_v", "hh_scale", "hh_lo", "w1_sum", "w1_v", "w1_k", "w1_exp", "w1_scale", "w1_lo"]
)

PER_TILE = (
    ["proj", "stats_a", "mean_a", "ve_a", "rstd_a", "centred", "res", "stats_b", "mean_b", "ve_b", "rstd_b",
     "xn", "turned", "xnT", "pre", "xg", "biased0", "biased1"]
    + [f"{n}{p}" for p in (0, 1) for n in (
        "rec_done", "pre_ready", "gates_ready", "fi_ready", "cell_ready", "tanhc_ready", "h_hi", "h_ready", "h_lo")]
    + ["hs_turned", "h_added", "ln_stats", "ln_mean", "ln_var", "ln_rstd", "xf_ready", "xf_turned", "xf_hi", "xf_lo"]
    + ["z_done", "z_ready", "logits_done", "top_found", "top_index", "neg_max", "tanh_logits",
       "one_minus", "one_minus_inv", "exps", "exp_sum", "exp_sum_inv", "gap", "gap_tanh", "weight1", "weight2",
       "index_f", "part1", "part2", "comb", "comb_turned", "combT_ready", "bias_done", "bias_added"]
    + [f"mm1_{e}" for e in range(NE)] + [f"gelu_{e}" for e in range(NE)]
    + [f"mm2_{e}" for e in range(NE)] + [f"acc_{e}" for e in range(NE)]
)


def audio_tower(nc, first, rows, affine, cols, xrest, we1, we2, out):
    with ExitStack() as ctx:
        def sb(name, shape, dt=F32):
            return ctx.enter_context(nc.sbuf_tensor(name, shape, dt))

        def bank(name):
            return ctx.enter_context(nc.psum_tensor(name, [P, 512], F32))

        def sem(name):
            return ctx.enter_context(nc.semaphore(name))

        first_sb = sb("first_sb", [P, A_COLS])
        xrest_sb = sb("xrest_sb", [P, X_COLS])
        rows_sb = sb("rows_sb", [NE, R_COLS])
        affine_sb = sb("affine_sb", [P, 2, D])
        cols_sb = sb("cols_sb", [P, C_COLS])
        we1_sb = sb("we1_sb", [P, W1])
        we2_sb = sb("we2_sb", [P, NE, HC, D])
        whh_hi = sb("whh_hi", [P, G4 * D], F16)
        whh_lo = sb("whh_lo", [P, G4 * D], F16)
        we1_hi = sb("we1_hi", [P, W1], F16)
        we1_lo = sb("we1_lo", [P, W1], F16)
        ones = sb("ones", [P, P])
        idle = sb("idle", [P, P], F16)
        neg_half = sb("neg_half", [P, 1])
        squares = sb("squares", [P, W1], F16)
        sumsq_hh = sb("sumsq_hh", [P, 1])
        sumsq_w1 = sb("sumsq_w1", [P, PARTS + 1])
        v_hh = sb("v_hh", [P, 1], U32)
        v_w1 = sb("v_w1", [P, 3], U32)
        scale_hh = sb("scale_hh", [P, 3], U32)
        scale_w1 = sb("scale_w1", [P, 2], U32)
        res = sb("res", [P, TILES, D])
        centred = sb("centred", [P, TILES, D])
        xn = sb("xn", [P, TILES, D])
        xnT = sb("xnT", [P, TILES, P])
        bn = sb("bn", [P, TILES, 6])
        mv = sb("mv", [P, TILES, 2])
        ve = sb("ve", [P, TILES])
        rstd = sb("rstd", [P, TILES])
        xg = sb("xg", [P, TILES, 2, G4, B])
        bias = sb("bias", [P, G4])
        cell = [sb(f"cell{p}", [P, 5, B]) for p in (0, 1)]
        pre = sb("pre", [P, G4, B])
        fi = sb("fi", [P, 2, B])
        tanhc = sb("tanhc", [P, B])
        h2 = sb("h2", [P, 2, B])
        h_hi = sb("h_hi", [P, 2, B], F16)
        h_lo = sb("h_lo", [P, 2, B], F16)
        lnbn = sb("lnbn", [P, 6])
        lnmv = sb("lnmv", [P, 2])
        lnve = sb("lnve", [P, 1])
        lnrs = sb("lnrs", [P, 1])
        xf = sb("xf", [P, D])
        xf_hi = sb("xf_hi", [P, 2, P], F16)
        xf_lo = sb("xf_lo", [P, 2, P], F16)
        zT = sb("zT", [GH + 1, P])
        top = sb("top", [P, NE])
        top_i = sb("top_i", [P, NE], U32)
        top_f = sb("top_f", [P, 2])
        nmax = sb("nmax", [P, 1])
        th = sb("th", [P, NE])
        den = sb("den", [P, NE])
        rden = sb("rden", [P, NE])
        ex = sb("ex", [P, NE])
        esum = sb("esum", [P, 1])
        rsum = sb("rsum", [P, 1])
        ngap = sb("ngap", [P, 1])
        tgap = sb("tgap", [P, 1])
        tw1 = sb("tw1", [P, 1])
        tw2 = sb("tw2", [P, 1])
        cp1 = sb("cp1", [P, NE])
        cp2 = sb("cp2", [P, NE])
        comb = sb("comb", [P, 2, NE])
        combT = sb("combT", [NE, P])
        hidT = [sb(f"hidT{k}", [P, HC, P]) for k in range(4)]

        hid_ps = [bank("hid0"), bank("hid1")]
        y_ps = [bank("y0"), bank("y1")]
        gate_ps = bank("gate_ps")
        turn_ps = bank("turn_ps")
        lg_ps = bank("lg_ps")
        cb_ps = bank("cb_ps")
        proj_ps = [ps[:, 0:D] for ps in (hid_ps[1], hid_ps[0], y_ps[0], y_ps[1], y_ps[0])]
        pre_ps = [gate_ps, hid_ps[0], y_ps[1], cb_ps, cb_ps]

        load = {n: sem(f"load_{n}") for n in LOADS}
        F = {n: sem(f"f_{n}") for n in FRONT}
        S = {n: sem(n) for n in PER_TILE}
        stored = sem("stored")

        ident = cols_sb[:, C_ID:C_ID + P]
        iota = cols_sb[:, C_IOTA:C_IOTA + NE]
        gamma, beta = affine_sb[:, 0], affine_sb[:, 1]
        unscale_hh = scale_hh[:, 2:3].bitcast(F32)
        down_w1 = scale_w1[:, 0:1].bitcast(F32)
        up_w1 = scale_w1[:, 1:2].bitcast(F32)
        wih_sb = cols_sb[:, C_WIH:]
        whh_sb = xrest_sb[:, X_WHH:]
        rec_ps = gate_ps[:, 0:G4 * B].rearrange("q (g b) -> q g b", g=G4)

        def by_gate(ps, g):
            return ps[:].rearrange("q (s g b) -> q g s b", s=2, g=G4)[:, g]

        block = ctx.enter_context(nc.Block())

        @block.sync
        def _(sp):
            sp.dma_start(first_sb[:], first).then_inc(load["first"], 16)
            sp.dma_start(rows_sb[:], rows).then_inc(load["rows"], 16)
            sp.dma_start(affine_sb[:].rearrange("q a d -> q (a d)"), affine.broadcast_to([P, 2 * D])
                         ).then_inc(load["affine"], 16)
            sp.dma_start(cols_sb[:], cols).then_inc(load["cols"], 16)
            sp.dma_start(xrest_sb[:], xrest).then_inc(load["xrest"], 16)
            sp.dma_start(we1_sb[:, 0:HALF1], we1[:, 0:HALF1]).then_inc(load["we1a"], 16)
            sp.dma_start(we1_sb[:, HALF1:], we1[:, HALF1:]).then_inc(load["we1b"], 16)
            h = NE // 2
            sp.dma_start(we2_sb[:, 0:h], we2[:, 0:h]).then_inc(load["we2a"], 16)
            sp.dma_start(we2_sb[:, h:NE], we2[:, h:NE]).then_inc(load["we2b"], 16)
            for t in range(TILES):
                sp.wait_ge(S[f"acc_{NE - 1}"], t + 1)
                sp.dma_start(out[:, 2 * t:2 * t + 2, :].rearrange("b p d -> p b d"), res[:, t, :]).then_inc(stored, 16)
            sp.wait_ge(stored, 16 * TILES)

        @block.gpsimd
        def _(pool):
            nc.gpsimd.memset(ones[:], 1.0).then_inc(F["ones"], 1)
            nc.gpsimd.memset(neg_half[:], -0.5).then_inc(F["neg_half"], 1)
            nc.gpsimd.memset(cell[0][:, 0, :], 0.0).then_inc(F["cell_zero"], 1)
            pool.wait_ge(F["cell_zero"], 1)
            nc.gpsimd.memset(zT[GH:GH + 1, :], 1.0).then_inc(F["z_one"], 1)
            pool.wait_ge(F["z_one"], 1)
            pool.wait_ge(F["neg_half"], 1)

            def rstd_of(t, ln):
                pool.wait_ge(S[f"ve_{ln}"], t + 1)
                nc.gpsimd.tensor_tensor(rstd[:, t:t + 1], ve[:, t:t + 1], neg_half[:], ALU.pow
                                        ).then_inc(S[f"rstd_{ln}"], 1)

            def ln_rstd(t):
                pool.wait_ge(S["ln_var"], t + 1)
                nc.gpsimd.tensor_tensor(lnrs[:], lnve[:], neg_half[:, 0:1], ALU.pow).then_inc(S["ln_rstd"], 1)

            def add_lstm_bias(t, p):
                pool.wait_ge(S["xg"], t + 1)
                nc.gpsimd.tensor_tensor(xg[:, t, p], xg[:, t, p], bias[:].unsqueeze(2).to_broadcast([P, G4, B]),
                                        ALU.add).then_inc(S[f"biased{p}"], 1)

            def hidden_low(t, p):
                pool.wait_ge(S[f"h_hi{p}"], t + 1)
                pool.wait_ge(S[f"h_ready{p}"], t + 1)
                if t >= 1:
                    pool.wait_ge(S[f"rec_done{1 - p}"], t)
                nc.gpsimd.tensor_tensor(h_lo[:, p, :], h2[:, p, :], h_hi[:, p, :], ALU.subtract
                                        ).then_inc(S[f"h_lo{p}"], 1)

            pool.wait_ge(load["cols"], 16)
            nc.gpsimd.tensor_tensor(bias[:], cols_sb[:, C_BIH:C_BIH + G4], cols_sb[:, C_BHH:C_BHH + G4], ALU.add
                                    ).then_inc(F["bias_sum"], 1)
            rstd_of(0, "a")
            pool.wait_ge(F["bias_sum"], 1)
            nc.gpsimd.tensor_scalar(bias[:, 1:], bias[:, 1:], 0.5, None, ALU.mult).then_inc(F["bias_half"], 1)
            pool.wait_ge(F["bias_half"], 1)
            rstd_of(0, "b")
            rstd_of(1, "a")
            add_lstm_bias(0, 1)
            rstd_of(1, "b")
            hidden_low(0, 0)
            rstd_of(2, "a")
            hidden_low(0, 1)
            ln_rstd(0)
            add_lstm_bias(1, 0)
            add_lstm_bias(1, 1)
            rstd_of(2, "b")
            hidden_low(1, 0)
            rstd_of(3, "a")
            rstd_of(3, "b")
            hidden_low(1, 1)
            add_lstm_bias(2, 0)
            rstd_of(4, "a")
            add_lstm_bias(2, 1)
            for t in range(TILES - 1):
                ln_rstd(t + 1)
                if t + 2 < TILES:
                    hidden_low(t + 2, 0)
                if t == 0:
                    rstd_of(4, "b")
                if t + 2 < TILES:
                    hidden_low(t + 2, 1)
                if t < 2:
                    add_lstm_bias(3 + t, 0)
                    add_lstm_bias(3 + t, 1)

        @block.tensor
        def _(pe):
            def chunks(t, k):
                c = (2 * t + k) * B
                return first_sb[:, c:c + 2 * B] if c < 2 * B else xrest_sb[:, c - 3 * B:c - B]

            def project(t):
                if t == 2:
                    pe.wait_ge(F["hh_v"], 1)
                elif t == 4:
                    pe.wait_ge(S["centred"], 3)
                pe.matmul(proj_ps[t], ones[0:1, :], rows_sb[0:1, R_TOKB:R_TOKB + D], start=True, stop=False)
                if t == 1:
                    for b in (0, 1):
                        lhs = first_sb[:, 2 * B:3 * B] if b == 0 else xrest_sb[:, 0:B]
                        pe.matmul(proj_ps[t][b * B:(b + 1) * B], lhs, first_sb[:, A_W:A_W + D],
                                  start=False, stop=False)
                else:
                    pe.matmul(proj_ps[t], chunks(t, 0), first_sb[:, A_W:A_W + D], start=False, stop=False)
                pe.matmul(proj_ps[t], chunks(t, 1), first_sb[:, A_W + D:A_W + 2 * D], start=False, stop=True
                          ).then_inc(S["proj"], 1)

            def warm(n):
                for _ in range(n):
                    pe.matmul(lg_ps[:, 384:512], idle[:], idle[:], start=True, stop=True)

            def turn_xn(t):
                pe.wait_ge(S["xn"], t + 1)
                if t == 0:
                    pe.wait_ge(load["cols"], 16)
                if t >= 1:
                    pe.wait_ge(S["xnT"], t)
                if t == TILES - 1:
                    pe.wait_ge(S["bias_added"], 1)
                pe.transpose(cb_ps[:, 2 * P:3 * P], xn[:, t, :], ident).then_inc(S["turned"], 1)

            def gate_inputs(t):
                pe.wait_ge(S["xnT"], t + 1)
                if t == 0:
                    pe.wait_ge(F["wih_scaled"], 1)
                elif t == 2:
                    pe.wait_ge(S["centred"], 4)
                for g in range(G4):
                    mm = pe.matmul(by_gate(pre_ps[t], g), wih_sb[:, g * D:(g + 1) * D], xnT[:, t, :],
                                   start=g == 0, stop=True, skip_group_check=True)
                mm.then_inc(S["pre"], 1)

            def recur(t, p):
                q, n = 1 - p, t + p
                pe.wait_ge(S[f"h_hi{q}"], n)
                if t == 0:
                    pe.wait_ge(F["hh_hi"], 1)
                    pe.wait_ge(F["hh_lo"], 1)
                    pe.wait_ge(S["xg"], 1)
                for g in range(G4):
                    for w in (whh_hi, whh_lo):
                        pe.matmul(rec_ps[:, g, :], w[:, g * D:(g + 1) * D], h_hi[:, q, :],
                                  start=g == 0 and w is whh_hi, stop=False, skip_group_check=True)
                pe.wait_ge(S[f"h_lo{q}"], n)
                for g in range(G4):
                    mm = pe.matmul(rec_ps[:, g, :], whh_hi[:, g * D:(g + 1) * D], h_lo[:, q, :],
                                   start=False, stop=True, skip_group_check=True)
                mm.then_inc(S[f"rec_done{p}"], 1)

            def turn_h(t):
                pe.wait_ge(S["h_ready1"], t + 1)
                if t >= 1:
                    pe.wait_ge(S["xf_lo"], t)
                pe.transpose(turn_ps[:, 0:P], h2[:].rearrange("q s b -> q (s b)"), ident).then_inc(S["hs_turned"], 1)

            def turn_xf(t):
                pe.wait_ge(S["xf_ready"], t + 1)
                pe.transpose(turn_ps[:, P:2 * P], xf[:], ident).then_inc(S["xf_turned"], 1)

            def three(dst, c0, c1, t):
                pe.matmul(dst, we1_hi[:, c0:c1], xf_hi[:, t % 2], start=True, stop=False)
                pe.matmul(dst, we1_hi[:, c0:c1], xf_lo[:, t % 2], start=False, stop=False)
                return pe.matmul(dst, we1_lo[:, c0:c1], xf_hi[:, t % 2], start=False, stop=True)

            def split_part(k):
                pe.wait_ge(F["w1_hi"], k + 1)
                pe.wait_ge(F["w1_lo"], k + 1)

            def gate_hidden(t):
                pe.wait_ge(S["xf_hi"], t + 1)
                pe.wait_ge(S["xf_lo"], t + 1)
                if t == 0:
                    split_part(0)
                if t >= 1:
                    pe.wait_ge(S["top_index"], t)
                three(lg_ps[0:GH, 0:P], 0, GH, t).then_inc(S["z_done"], 1)

            def gate_logits(t):
                pe.wait_ge(S["z_ready"], t + 1)
                pe.matmul(lg_ps[:, P:P + NE], zT[:], cols_sb[0:GH + 1, C_GW2:C_GW2 + NE], start=True, stop=True
                          ).then_inc(S["logits_done"], 1)

            def turn_comb(t):
                pe.wait_ge(S["comb"], t + 1)
                if t <= 1:
                    pe.wait_ge(S["xg"], t + 4)
                if t >= 1:
                    pe.wait_ge(S["bias_added"], t)
                pe.transpose(cb_ps[0:NE, 0:P], comb[:, t % 2], ident).then_inc(S["comb_turned"], 1)

            def expert_bias(t):
                pe.wait_ge(S["combT_ready"], t + 1)
                pe.matmul(cb_ps[:, P:2 * P], combT[:], rows_sb[:, R_BE2:R_BE2 + D], start=True, stop=True
                          ).then_inc(S["bias_done"], 1)

            def mm1(t, e):
                if e >= 2:
                    pe.wait_ge(S[f"gelu_{e - 2}"], t + 1)
                elif t >= 1:
                    pe.wait_ge(S[f"gelu_{NE - 2 + e}"], t)
                else:
                    pe.wait_ge(S["xg"], 2)
                if t == 0 and e % 2 == 0:
                    split_part(e // 2)
                for j in range(HC):
                    c = GH + (HC * e + j) * P
                    mm = three(hid_ps[e % 2][:, j * P:(j + 1) * P], c, c + P, t)
                mm.then_inc(S[f"mm1_{e}"], 1)

            def mm2(t, e):
                pe.wait_ge(S[f"gelu_{e}"], t + 1)
                if e % 2 == 0 and e >= 4:
                    pe.wait_ge(S[f"acc_{e - 3}"], t + 1)
                elif e % 2 == 0 and t >= 1:
                    pe.wait_ge(S[f"acc_{NE - 3 + e}"], t)
                elif e == 2:
                    pe.wait_ge(S["xg"], 3)
                elif e == 0:
                    pe.wait_ge(S["centred"], TILES)
                    pe.wait_ge(load["we2a"], 16)
                if e == 4 and t == 0:
                    pe.wait_ge(load["we2b"], 16)
                for j in range(HC):
                    mm = pe.matmul(y_ps[e // 2 % 2][:, (e % 2) * D:(e % 2 + 1) * D], hidT[e % 4][:, j, :],
                                   we2_sb[:, e, j, :], start=j == 0, stop=j == 1)
                mm.then_inc(S[f"mm2_{e}"], 1)

            pe.wait_ge(F["idle"], 1)
            pe.wait_ge(F["ones"], 1)
            pe.wait_ge(load["first"], 16)
            pe.wait_ge(load["rows"], 16)
            project(0)
            warm(16)
            pe.wait_ge(load["xrest"], 16)
            project(1)
            pe.wait_ge(F["sq_hh"], 1)
            pe.matmul(y_ps[0][:, 511:512], ones[:], sumsq_hh[:], start=True, stop=True).then_inc(F["norm_hh"], 1)
            warm(12)
            turn_xn(0)
            warm(4)
            gate_inputs(0)
            warm(13)
            project(2)
            project(3)
            recur(0, 1)
            warm(14)
            warm(4)
            turn_xn(1)
            turn_h(0)
            gate_inputs(1)
            recur(1, 0)
            project(4)
            turn_xf(0)
            warm(16)
            gate_hidden(0)
            recur(1, 1)
            gate_logits(0)
            turn_xn(2)

            def iteration(t):
                before, now, after, lstm = t >= 1, t < TILES, t + 1 < TILES, t + 2 < TILES
                if now:
                    mm1(t, 0)
                if t == 0:
                    gate_inputs(2)
                    mm1(0, 1)
                if after:
                    turn_h(t + 1)
                if 1 <= t < TILES:
                    mm1(t, 1)
                if before:
                    mm2(t - 1, 6)
                if lstm:
                    recur(t + 2, 0)
                if before:
                    mm2(t - 1, 7)
                if now:
                    mm1(t, 2)
                    mm1(t, 3)
                if t <= 1:
                    turn_xn(t + 3)
                if now:
                    mm2(t, 0)
                if t == 0:
                    mm1(t, 4)
                if now:
                    mm2(t, 1)
                if after:
                    turn_xf(t + 1)
                if 1 <= t < TILES:
                    mm1(t, 4)
                if now:
                    mm1(t, 5)
                    if t <= 1:
                        gate_inputs(t + 3)
                    mm2(t, 2)
                if after:
                    gate_hidden(t + 1)
                if lstm:
                    recur(t + 2, 1)
                if now:
                    mm2(t, 3)
                if after:
                    gate_logits(t + 1)
                if now:
                    turn_comb(t)
                    mm1(t, 6)
                    mm1(t, 7)
                    mm2(t, 4)
                    expert_bias(t)
                    mm2(t, 5)

            for t in range(TILES + 1):
                iteration(t)

        @block.scalar
        def _(act):
            act.wait_ge(F["neg_half"], 1)
            nc.scalar.activation(tgap[:], neg_half[:], ACT.Gelu).then_inc(F["table"], 1)

            def xnT_copy(t):
                act.wait_ge(S["turned"], t + 1)
                nc.scalar.copy(xnT[:, t, :], cb_ps[:, 2 * P:3 * P]).then_inc(S["xnT"], 1)

            def xg_copy(t):
                act.wait_ge(S["pre"], t + 1)
                if t == 0:
                    act.wait_ge(S["pre_ready0"], 1)
                    nc.scalar.copy(xg[:, 0, 1].rearrange("q g b -> q (g b)"), gate_ps[:, G4 * B:]
                                   ).then_inc(S["xg"], 1)
                else:
                    nc.scalar.copy(xg[:, t].rearrange("q s g b -> q (s g b)"), pre_ps[t][:]).then_inc(S["xg"], 1)

            def gates(t, p, src, ready, n):
                act.wait_ge(ready, n)
                if t >= 1 or p == 1:
                    act.wait_ge(S[f"h_ready{1 - p}"], t + p)
                nc.scalar.activation(cell[p][:, 1:5, :], src, ACT.Tanh).then_inc(S[f"gates_ready{p}"], 1)

            def tanh_cell(t, p):
                act.wait_ge(S[f"cell_ready{p}"], t + 1)
                if t >= 1 or p == 1:
                    act.wait_ge(S[f"h_ready{1 - p}"], t + p)
                nc.scalar.activation(tanhc[:], cell[1 - p][:, 0, :], ACT.Tanh, scale=0.5
                                     ).then_inc(S[f"tanhc_ready{p}"], 1)

            act.wait_ge(load["cols"], 16)
            nc.scalar.mul(wih_sb[:, D:], wih_sb[:, D:], 0.5).then_inc(F["wih_scaled"], 1)
            act.wait_ge(load["xrest"], 16)
            nc.scalar.activation(squares[:, 0:G4 * D], whh_sb, ACT.Square, accum_out=sumsq_hh[:]
                                 ).then_inc(F["sq_hh"], 1)
            act.wait_ge(F["hh_scale"], 1)
            nc.scalar.activation(whh_hi[:, 0:D], whh_sb[:, 0:D], ACT.Copy, scale=scale_hh[:, 0:1].bitcast(F32))
            xnT_copy(0)
            nc.scalar.activation(whh_hi[:, D:], whh_sb[:, D:], ACT.Copy, scale=scale_hh[:, 1:2].bitcast(F32)
                                 ).then_inc(F["hh_hi"], 1)

            def square_w1(k):
                c0, c1 = PART_ENDS[k:k + 2]
                if k % (PARTS // 2) == 0:
                    act.wait_ge(load["we1b" if k else "we1a"], 16)
                if k == 0:
                    act.wait_ge(F["sq_hh"], 1)
                else:
                    act.wait_ge(F["sq_w1"], k)
                nc.scalar.activation(squares[:, 0:c1 - c0], we1_sb[:, c0:c1], ACT.Square,
                                     accum_out=sumsq_w1[:, k:k + 1]).then_inc(F["sq_w1"], 1)

            def w1_high(k):
                c0, c1 = PART_ENDS[k:k + 2]
                if k == 0:
                    act.wait_ge(F["w1_scale"], 1)
                nc.scalar.activation(we1_hi[:, c0:c1], we1_sb[:, c0:c1], ACT.Copy, scale=down_w1
                                     ).then_inc(F["w1_hi"], 1)

            def xf_high(t):
                act.wait_ge(S["xf_turned"], t + 1)
                if t >= 2:
                    act.wait_ge(S[f"mm1_{NE - 1}"], t - 1)
                nc.scalar.activation(xf_hi[:, t % 2], turn_ps[:, P:2 * P], ACT.Copy, scale=up_w1).then_inc(S["xf_hi"], 1)

            def gelu(t, e):
                act.wait_ge(S[f"mm1_{e}"], t + 1)
                if e >= 4:
                    act.wait_ge(S[f"mm2_{e - 4}"], t + 1)
                elif t >= 1:
                    act.wait_ge(S[f"mm2_{e + 4}"], t)
                for j in range(HC):
                    c = C_BE1 + HC * e + j
                    a = nc.scalar.activation(hidT[e % 4][:, j, :], hid_ps[e % 2][:, j * P:(j + 1) * P], ACT.Gelu,
                                             bias=cols_sb[:, c:c + 1], scale=W1_BACK)
                a.then_inc(S[f"gelu_{e}"], 1)

            def z(t):
                act.wait_ge(S["z_done"], t + 1)
                if t >= 1:
                    act.wait_ge(S["logits_done"], t)
                nc.scalar.activation(zT[0:GH, :], lg_ps[0:GH, 0:P], ACT.Relu, bias=cols_sb[0:GH, C_GB1:C_GB1 + 1],
                                     scale=W1_BACK).then_inc(S["z_ready"], 1)

            def tanh_logits(t):
                act.wait_ge(S["neg_max"], t + 1)
                nc.scalar.activation(th[:], top[:], ACT.Tanh, bias=nmax[:], scale=0.5).then_inc(S["tanh_logits"], 1)

            def tanh_gap(t):
                act.wait_ge(S["gap"], t + 1)
                nc.scalar.activation(tgap[:], ngap[:], ACT.Tanh, scale=-0.5).then_inc(S["gap_tanh"], 1)

            def combT_copy(t):
                act.wait_ge(S["comb_turned"], t + 1)
                if t >= 1:
                    act.wait_ge(S["bias_done"], t)
                nc.scalar.copy(combT[:], cb_ps[0:NE, 0:P]).then_inc(S["combT_ready"], 1)

            square_w1(0)
            square_w1(1)
            gates(0, 0, pre[:], S["pre_ready0"], 1)
            xg_copy(0)
            tanh_cell(0, 0)
            square_w1(2)
            square_w1(3)
            gates(0, 1, pre[:], S["pre_ready1"], 1)
            xnT_copy(1)
            tanh_cell(0, 1)
            w1_high(0)
            xg_copy(1)
            w1_high(1)
            gates(1, 0, pre[:], S["pre_ready0"], 2)
            xf_high(0)
            tanh_cell(1, 0)
            z(0)
            w1_high(2)
            xnT_copy(2)
            gates(1, 1, pre[:], S["pre_ready1"], 2)
            tanh_logits(0)
            gelu(0, 0)
            tanh_cell(1, 1)
            xg_copy(2)
            gelu(0, 1)

            def iteration(t):
                after, lstm = t + 1 < TILES, t + 2 < TILES
                if t >= 1:
                    gelu(t, 0)
                tanh_gap(t)
                if t >= 1:
                    gelu(t, 1)
                if t == 0:
                    gelu(t, 2)
                if lstm:
                    gates(t + 2, 0, pre[:], S["pre_ready0"], t + 3)
                if t == 0:
                    w1_high(3)
                if t >= 1:
                    gelu(t, 2)
                if t <= 1:
                    xnT_copy(t + 3)
                gelu(t, 3)
                if lstm:
                    tanh_cell(t + 2, 0)
                if after:
                    xf_high(t + 1)
                gelu(t, 4)
                if t <= 1:
                    xg_copy(t + 3)
                if after:
                    z(t + 1)
                gelu(t, 5)
                if lstm:
                    gates(t + 2, 1, pre[:], S["pre_ready1"], t + 3)
                if t >= 1:
                    combT_copy(t)
                if t == 0:
                    combT_copy(t)
                if after:
                    tanh_logits(t + 1)
                gelu(t, 6)
                if lstm:
                    tanh_cell(t + 2, 1)
                gelu(t, 7)

            for t in range(TILES):
                iteration(t)

        @block.vector
        def _(dve):
            def centre_scale(dst, src, mean, rs):
                return nc.vector.tensor_scalar(dst, src, mean, rs, ALU.subtract, ALU.mult)

            def forget_input(t, p):
                dve.wait_ge(S[f"gates_ready{p}"], t + 1)
                if t == 0 and p == 0:
                    dve.wait_ge(F["cell_zero"], 1)
                nc.vector.scalar_tensor_tensor(fi[:], cell[p][:, 2:4, :], 1.0, cell[p][:, 0:2, :],
                                               ALU.add, ALU.mult).then_inc(S[f"fi_ready{p}"], 1)

            def new_cell(t, p):
                dve.wait_ge(S[f"fi_ready{p}"], t + 1)
                nc.vector.scalar_tensor_tensor(cell[1 - p][:, 0, :], fi[:, 0, :], 0.5, fi[:, 1, :],
                                               ALU.mult, ALU.add).then_inc(S[f"cell_ready{p}"], 1)

            def hidden(t, p):
                dve.wait_ge(S[f"tanhc_ready{p}"], t + 1)
                if t >= 1:
                    dve.wait_ge(S[f"rec_done{1 - p}"], t)
                    dve.wait_ge(S[f"h_lo{p}"], t)
                    dve.wait_ge(S["hs_turned"], t)
                o = cell[p][:, 4, :]
                if p == 0:
                    nc.vector.scalar_tensor_tensor(h_hi[:, p, :], o, 1.0, tanhc[:], ALU.add, ALU.mult
                                                   ).then_inc(S[f"h_hi{p}"], 1)
                nc.vector.scalar_tensor_tensor(h2[:, p, :], o, 1.0, tanhc[:], ALU.add, ALU.mult
                                               ).then_inc(S[f"h_ready{p}"], 1)
                if p == 1:
                    nc.vector.scalar_tensor_tensor(h_hi[:, p, :], o, 1.0, tanhc[:], ALU.add, ALU.mult
                                                   ).then_inc(S[f"h_hi{p}"], 1)

            def add_pre(t, p):
                dve.wait_ge(S[f"biased{p}"], t + p)
                n = t if p == 0 else t + 1
                dve.wait_ge(S[f"rec_done{p}"], n)
                if t >= 1:
                    dve.wait_ge(S[f"gates_ready{1 - p}"], t + p)
                nc.vector.scalar_tensor_tensor(pre[:], rec_ps, unscale_hh, xg[:, t, p], ALU.mult, ALU.add
                                               ).then_inc(S[f"pre_ready{p}"], 1)

            def first_pre():
                dve.wait_ge(S["pre"], 1)
                dve.wait_ge(F["bias_half"], 1)
                nc.vector.tensor_tensor(pre[:], rec_ps, bias[:].unsqueeze(2).to_broadcast([P, G4, B]), ALU.add
                                        ).then_inc(S["pre_ready0"], 1)

            def front(t, stage):
                def named(ins, name):
                    ins.then_inc(S[name], 1)

                def after(name):
                    dve.wait_ge(S[name], t + 1)

                ps, row = proj_ps[t], res[:, t, :]
                mean, var, rs = mv[:, t, 0:1], mv[:, t, 1:2], rstd[:, t:t + 1]
                if stage == 0:
                    after("proj")
                    named(nc.vector.bn_stats(bn[:, t, :], ps), "stats_a")
                elif stage == 1:
                    after("stats_a")
                    named(nc.vector.bn_aggr(mv[:, t, :], bn[:, t, :]), "mean_a")
                elif stage == 2:
                    after("mean_a")
                    named(nc.vector.tensor_scalar(ve[:, t:t + 1], var, TOK_EPS, None, ALU.add), "ve_a")
                    dve.wait_ge(load["affine"], 16)
                    named(nc.vector.scalar_tensor_tensor(centred[:, t, :], ps, mean, gamma, ALU.subtract, ALU.mult),
                          "centred")
                elif stage == 3:
                    after("rstd_a")
                    after("centred")
                    named(nc.vector.scalar_tensor_tensor(row, centred[:, t, :], rs, beta, ALU.mult, ALU.add), "res")
                elif stage == 4:
                    after("res")
                    named(nc.vector.bn_stats(bn[:, t, :], row), "stats_b")
                elif stage == 5:
                    after("stats_b")
                    named(nc.vector.bn_aggr(mv[:, t, :], bn[:, t, :]), "mean_b")
                elif stage == 6:
                    after("mean_b")
                    named(nc.vector.tensor_scalar(ve[:, t:t + 1], var, LN_EPS, None, ALU.add), "ve_b")
                else:
                    after("rstd_b")
                    named(centre_scale(xn[:, t, :], row, mean, rs), "xn")

            def fronts(*stages):
                for t, stage in stages:
                    front(t, stage)

            nc.vector.memset(idle[:], 1.0).then_inc(F["idle"], 1)
            fronts((0, 0), (0, 1), (0, 2), (0, 3), (0, 4), (0, 5), (0, 6))
            dve.wait_ge(F["norm_hh"], 1)
            nc.vector.tensor_scalar(v_hh[:], y_ps[0][:, 511:512].bitcast(U32), 24, None,
                                    ALU.logical_shift_right).then_inc(F["hh_v"], 1)
            front(0, 7)
            dve.wait_ge(F["hh_v"], 1)
            for k, (sign, bits) in enumerate(((-1, HH_TO - EXP1), (-1, HH_TO - 2 * EXP1), (1, HH_BACK))):
                last = nc.vector.tensor_scalar(scale_hh[:, k:k + 1], v_hh[:], sign * EXP1, bits, ALU.mult, ALU.add)
            last.then_inc(F["hh_scale"], 1)

            def hh_low(g):
                if g == 0:
                    dve.wait_ge(F["hh_hi"], 1)
                k = min(g, 1)
                return nc.vector.scalar_tensor_tensor(whh_lo[:, g * D:(g + 1) * D], whh_sb[:, g * D:(g + 1) * D],
                                                      scale_hh[:, k:k + 1].bitcast(F32), whh_hi[:, g * D:(g + 1) * D],
                                                      ALU.mult, ALU.subtract)

            def w1_sum():
                dve.wait_ge(F["sq_w1"], PARTS)
                nc.vector.tensor_reduce(sumsq_w1[:, PARTS:], sumsq_w1[:, 0:PARTS], AX.X, ALU.add
                                        ).then_inc(F["w1_sum"], 1)

            def w1_v():
                dve.wait_ge(F["w1_sum"], 1)
                nc.vector.tensor_scalar(v_w1[:, 0:1], sumsq_w1[:, PARTS:].bitcast(U32), 24, None,
                                        ALU.logical_shift_right).then_inc(F["w1_v"], 1)

            def w1_k():
                dve.wait_ge(F["w1_v"], 1)
                nc.vector.tensor_scalar(v_w1[:, 1:2], v_w1[:, 0:1], -W1_FROM, 0.0, ALU.add, ALU.max
                                        ).then_inc(F["w1_k"], 1)

            def w1_exp():
                dve.wait_ge(F["w1_k"], 1)
                nc.vector.tensor_scalar(v_w1[:, 2:3], v_w1[:, 1:2], W1_MOST, EXP1, ALU.min, ALU.mult
                                        ).then_inc(F["w1_exp"], 1)

            def w1_scale():
                dve.wait_ge(F["w1_exp"], 1)
                for k, (sign, bits) in enumerate(((-1.0, (127 + W1_UP) * EXP1), (1.0, 127 * EXP1))):
                    last = nc.vector.tensor_scalar(scale_w1[:, k:k + 1], v_w1[:, 2:3], sign, bits, ALU.mult, ALU.add)
                last.then_inc(F["w1_scale"], 1)

            fronts((1, 0), (1, 1), (1, 2))
            hh_low(0)
            hh_low(1)
            hh_low(2)
            first_pre()
            front(1, 3)
            hh_low(3).then_inc(F["hh_lo"], 1)
            forget_input(0, 0)
            front(1, 4)
            new_cell(0, 0)
            fronts((1, 5), (1, 6), (2, 0))
            hidden(0, 0)
            fronts((3, 0), (2, 1), (2, 2))
            w1_sum()
            add_pre(0, 1)
            w1_v()
            fronts((2, 3), (1, 7))
            forget_input(0, 1)
            w1_k()
            w1_exp()
            new_cell(0, 1)
            front(2, 4)
            hidden(0, 1)
            w1_scale()

            def w1_low(k):
                c0, c1 = PART_ENDS[k:k + 2]
                dve.wait_ge(F["w1_hi"], k + 1)
                nc.vector.scalar_tensor_tensor(we1_lo[:, c0:c1], we1_sb[:, c0:c1], down_w1, we1_hi[:, c0:c1],
                                               ALU.mult, ALU.subtract).then_inc(F["w1_lo"], 1)

            def add_h(t):
                dve.wait_ge(S["hs_turned"], t + 1)
                nc.vector.scalar_tensor_tensor(res[:, t, :], turn_ps[:, 0:P], 0.5, res[:, t, :], ALU.mult, ALU.add
                                               ).then_inc(S["h_added"], 1)

            def ln_moments(t):
                dve.wait_ge(S["h_added"], t + 1)
                nc.vector.bn_stats(lnbn[:], res[:, t, :]).then_inc(S["ln_stats"], 1)

            def ln_mean(t):
                dve.wait_ge(S["ln_stats"], t + 1)
                nc.vector.bn_aggr(lnmv[:], lnbn[:]).then_inc(S["ln_mean"], 1)

            def ln_var(t):
                dve.wait_ge(S["ln_mean"], t + 1)
                nc.vector.tensor_scalar(lnve[:], lnmv[:, 1:2], LN_EPS, None, ALU.add).then_inc(S["ln_var"], 1)

            def ln_out(t):
                dve.wait_ge(S["ln_rstd"], t + 1)
                if t >= 1:
                    dve.wait_ge(S["xf_turned"], t)
                centre_scale(xf[:], res[:, t, :], lnmv[:, 0:1], lnrs[:]).then_inc(S["xf_ready"], 1)

            def xf_low(t):
                dve.wait_ge(S["xf_hi"], t + 1)
                if t >= 2:
                    dve.wait_ge(S[f"mm1_{NE - 1}"], t - 1)
                nc.vector.scalar_tensor_tensor(xf_lo[:, t % 2], turn_ps[:, P:2 * P], up_w1, xf_hi[:, t % 2],
                                               ALU.mult, ALU.subtract).then_inc(S["xf_lo"], 1)

            def top_sort(t):
                dve.wait_ge(S["logits_done"], t + 1)
                nc.vector.max(top[:], lg_ps[:, P:P + NE]).then_inc(S["top_found"], 1)

            def top_where(t):
                dve.wait_ge(S["top_found"], t + 1)
                nc.vector.tensor_scalar(nmax[:], top[:, 0:1], -0.5, None, ALU.mult).then_inc(S["neg_max"], 1)
                nc.vector.max_index(top_i[:], top[:], lg_ps[:, P:P + NE]).then_inc(S["top_index"], 1)

            def softmax_1(t):
                dve.wait_ge(S["tanh_logits"], t + 1)
                nc.vector.tensor_scalar(den[:], th[:], -1.0, 1.0, ALU.mult, ALU.add).then_inc(S["one_minus"], 1)

            def softmax_2(t):
                dve.wait_ge(S["one_minus"], t + 1)
                nc.vector.reciprocal(rden[:], den[:]).then_inc(S["one_minus_inv"], 1)

            def softmax_3(t):
                dve.wait_ge(S["one_minus_inv"], t + 1)
                nc.vector.scalar_tensor_tensor(ex[:], th[:], 1.0, rden[:], ALU.add, ALU.mult).then_inc(S["exps"], 1)

            def softmax_4(t):
                dve.wait_ge(S["exps"], t + 1)
                nc.vector.tensor_reduce(esum[:], ex[:], AX.X, ALU.add).then_inc(S["exp_sum"], 1)

            def softmax_5(t):
                dve.wait_ge(S["exp_sum"], t + 1)
                nc.vector.reciprocal(rsum[:], esum[:]).then_inc(S["exp_sum_inv"], 1)

            def softmax_6(t):
                dve.wait_ge(S["exp_sum_inv"], t + 1)
                nc.vector.scalar_tensor_tensor(ngap[:], ex[:, 1:2], -1.0, rsum[:], ALU.add, ALU.mult
                                               ).then_inc(S["gap"], 1)
                dve.wait_ge(S["top_index"], t + 1)
                nc.vector.tensor_copy(top_f[:], top_i[:, 0:2]).then_inc(S["index_f"], 1)

            def combine_1(t):
                dve.wait_ge(S["gap_tanh"], t + 1)
                nc.vector.tensor_scalar(tw1[:], tgap[:], 0.5, 0.5, ALU.mult, ALU.add).then_inc(S["weight1"], 1)
                nc.vector.tensor_scalar(tw2[:], tgap[:], -0.5, 0.5, ALU.mult, ALU.add).then_inc(S["weight2"], 1)

            def combine_2(t):
                dve.wait_ge(S["index_f"], t + 1)
                dve.wait_ge(S["weight1"], t + 1)
                nc.vector.tensor_scalar(cp1[:], iota, top_f[:, 0:1], tw1[:], ALU.is_equal, ALU.mult
                                        ).then_inc(S["part1"], 1)
                dve.wait_ge(S["weight2"], t + 1)
                nc.vector.tensor_scalar(cp2[:], iota, top_f[:, 1:2], tw2[:], ALU.is_equal, ALU.mult
                                        ).then_inc(S["part2"], 1)

            def combine_3(t):
                dve.wait_ge(S["part1"], t + 1)
                dve.wait_ge(S["part2"], t + 1)
                if t >= 2:
                    dve.wait_ge(S[f"acc_{NE - 1}"], t - 1)
                    dve.wait_ge(S["comb_turned"], t - 1)
                nc.vector.tensor_tensor(comb[:, t % 2], cp1[:], cp2[:], ALU.add).then_inc(S["comb"], 1)

            def add_expert_bias(t):
                dve.wait_ge(S["bias_done"], t + 1)
                dve.wait_ge(S["acc_3"], t + 1)
                nc.vector.tensor_tensor(res[:, t, :], res[:, t, :], cb_ps[:, P:2 * P], ALU.add
                                        ).then_inc(S["bias_added"], 1)

            def accumulate(t, e):
                dve.wait_ge(S[f"mm2_{e | 1}"], t + 1)
                if e == 4:
                    dve.wait_ge(S["bias_added"], t + 1)
                elif e >= 1:
                    dve.wait_ge(S[f"acc_{e - 1}"], t + 1)
                else:
                    dve.wait_ge(S["comb"], t + 1)
                nc.vector.scalar_tensor_tensor(res[:, t, :], y_ps[e // 2 % 2][:, (e % 2) * D:(e % 2 + 1) * D],
                                               comb[:, t % 2, e:e + 1], res[:, t, :], ALU.mult, ALU.add
                                               ).then_inc(S[f"acc_{e}"], 1)

            add_h(0)
            ln_moments(0)
            front(3, 1)
            ln_mean(0)
            front(2, 5)
            ln_var(0)
            w1_low(0)
            ln_out(0)
            fronts((2, 6), (4, 0))
            add_pre(1, 0)
            front(3, 2)
            forget_input(1, 0)
            front(2, 7)
            new_cell(1, 0)
            front(4, 1)
            xf_low(0)
            hidden(1, 0)
            front(4, 2)
            w1_low(1)
            add_pre(1, 1)
            top_sort(0)
            front(3, 3)
            top_where(0)
            forget_input(1, 1)
            front(3, 4)
            new_cell(1, 1)
            front(3, 5)
            softmax_1(0)
            front(3, 6)
            softmax_2(0)
            hidden(1, 1)
            softmax_3(0)
            softmax_4(0)
            front(3, 7)
            softmax_5(0)

            def iteration(t):
                before, now, after, lstm = t >= 1, t < TILES, t + 1 < TILES, t + 2 < TILES
                if after:
                    add_h(t + 1)
                if now:
                    softmax_6(t)
                if before:
                    accumulate(t - 1, 5)
                if after:
                    ln_moments(t + 1)
                if now:
                    combine_1(t)
                if after:
                    ln_mean(t + 1)
                if lstm:
                    add_pre(t + 2, 0)
                if after:
                    ln_var(t + 1)
                if t == 0:
                    w1_low(2)
                    ln_out(t + 1)
                if now:
                    combine_2(t)
                if before:
                    accumulate(t - 1, 6)
                if lstm:
                    forget_input(t + 2, 0)
                if t >= 1 and after:
                    ln_out(t + 1)
                if lstm:
                    new_cell(t + 2, 0)
                if t >= 1 and now:
                    combine_3(t)
                if before:
                    accumulate(t - 1, 7)
                if lstm:
                    hidden(t + 2, 0)
                if t == 0:
                    combine_3(t)
                if now:
                    accumulate(t, 0)
                if after:
                    xf_low(t + 1)
                if now:
                    accumulate(t, 1)
                if t == 0:
                    w1_low(3)
                if lstm:
                    add_pre(t + 2, 1)
                if t >= 1 and after:
                    top_sort(t + 1)
                if now:
                    accumulate(t, 2)
                if t == 0:
                    front(4, 3)
                    top_sort(t + 1)
                if after:
                    top_where(t + 1)
                if lstm:
                    forget_input(t + 2, 1)
                if now:
                    accumulate(t, 3)
                if after:
                    softmax_1(t + 1)
                if lstm:
                    new_cell(t + 2, 1)
                if after:
                    softmax_2(t + 1)
                if t == 0:
                    front(4, 4)
                    softmax_3(t + 1)
                    front(4, 5)
                if now:
                    add_expert_bias(t)
                if t == 0:
                    front(4, 6)
                if lstm:
                    hidden(t + 2, 1)
                if t >= 1 and after:
                    softmax_3(t + 1)
                if after:
                    softmax_4(t + 1)
                if now:
                    accumulate(t, 4)
                if after:
                    softmax_5(t + 1)
                if t == 0:
                    front(4, 7)

            for t in range(TILES + 1):
                iteration(t)


def kernel(x, L0_tok_W, L0_tok_b, L0_tok_gamma, L0_tok_beta, L0_attn_W_ih, L0_attn_W_hh, L0_attn_b_ih,
           L0_attn_b_hh, L0_ffn_gw1, L0_ffn_gb1, L0_ffn_gw2, L0_ffn_gb2, L0_ffn_we1, L0_ffn_be1, L0_ffn_we2,
           L0_ffn_be2):
    import numpy as np
    import concourse.bacc as bacc
    from concourse.bass_utils import run_bass_kernel_spmd

    f = np.float32
    order = (2, 1, 0, 3)

    def by_gate(a):
        return np.concatenate([np.asarray(a).reshape(4, D, -1)[g] for g in order], axis=0)

    xs = np.asarray(x).reshape(B, -1)[:, :CHUNKS * STRIDE].reshape(B, CHUNKS, STRIDE).transpose(2, 1, 0)
    b_ih, b_hh = by_gate(L0_attn_b_ih).reshape(4, D), by_gate(L0_attn_b_hh).reshape(4, D)
    cols = np.zeros((P, C_COLS), f)
    cols[:, C_ID:C_ID + P] = np.eye(P, dtype=f)
    cols[:, C_WIH:] = by_gate(L0_attn_W_ih).T
    cols[:, C_BIH:C_BIH + G4] = b_ih.T
    cols[:, C_BHH:C_BHH + G4] = b_hh.T
    cols[:, C_BE1:C_BE1 + NE * HC] = np.asarray(L0_ffn_be1).reshape(NE * HC, P).T
    cols[:, C_IOTA:C_IOTA + NE] = np.arange(NE, dtype=f)
    cols[:GH, C_GB1] = np.asarray(L0_ffn_gb1)
    cols[:GH, C_GW2:C_GW2 + NE] = np.asarray(L0_ffn_gw2)
    cols[GH, C_GW2:C_GW2 + NE] = np.asarray(L0_ffn_gb2)
    rows = np.zeros((NE, R_COLS), f)
    rows[:, R_BE2:R_BE2 + D] = np.asarray(L0_ffn_be2)
    rows[0, R_TOKB:R_TOKB + D] = np.asarray(L0_tok_b)
    we1 = np.asarray(L0_ffn_we1).transpose(1, 0, 2).reshape(D, W1 - GH)
    xs = xs.reshape(P, CHUNKS * B)
    wtok = np.asarray(L0_tok_W).reshape(2, P, D).transpose(1, 0, 2).reshape(P, 2 * D)
    arrays = {
        "first": np.concatenate([xs[:, :3 * B], wtok], axis=1),
        "rows": rows,
        "affine": np.concatenate([np.asarray(L0_tok_gamma), np.asarray(L0_tok_beta)]).reshape(1, 2 * D),
        "cols": cols,
        "xrest": np.concatenate([xs[:, 3 * B:], by_gate(L0_attn_W_hh).T], axis=1),
        "we1": np.concatenate([np.asarray(L0_ffn_gw1), we1], axis=1),
        "we2": np.asarray(L0_ffn_we2).reshape(NE, HC, P, D).transpose(2, 0, 1, 3),
    }
    arrays = {n: np.ascontiguousarray(a) for n, a in arrays.items()}
    nc = bacc.Bacc("TRN2", target_bir_lowering=False, num_devices=1)
    args = [nc.dram_tensor(n, a.shape, F32, kind="ExternalInput").ap() for n, a in arrays.items()]
    out = nc.dram_tensor("out", (B, PATCHES, D), F32, kind="ExternalOutput").ap()
    audio_tower(nc, *args, out)
    got = run_bass_kernel_spmd(nc, [arrays], core_ids=[0])
    return got.results[0]["out"]
```
